# Optimizing a Trainium2 kernel written in Bass

```python
import numpy as np
import jax
import jax.numpy as jnp

def _softmax(x, axis=-1):
    return jax.nn.softmax(x, axis=axis)

def _gelu(x):
    return jax.nn.gelu(x, approximate=True)

def _silu(x):
    return jax.nn.silu(x)

def _sigmoid(x):
    return jax.nn.sigmoid(x)

def _layernorm(x, axis=-1, eps=1e-05):
    m = jnp.mean(x, axis=axis, keepdims=True)
    v = jnp.var(x, axis=axis, keepdims=True)
    return (x - m) / jnp.sqrt(v + eps)

def _scatter_add(tgt, idx, src, axis=0):
    return tgt.at[idx].add(src)

def _segment_sum(src, seg, n):
    return jax.ops.segment_sum(src, seg, n)
kernel_name = 'mk_seq_postln_d2_jaxref_r8_2c5c12'

def setup_inputs(seed: int=0):
    np.random.seed(seed)
    _w = jnp.asarray

    def _L0_attn_setup():
        import jax, jax.numpy as jnp
        import numpy as np
        D_MODEL = 128
        B, T = (4, 512)
        LN_EPS = 1e-05
        DEN_EPS = 1e-06
        key = jax.random.key(seed)
        ks = jax.random.split(key, 10)
        s = 1.0 / np.sqrt(D_MODEL)
        return {'x': jax.random.normal(ks[0], (B, T, D_MODEL), dtype=jnp.float32), 'w_qkv': jax.random.normal(ks[1], (D_MODEL, 3 * D_MODEL), dtype=jnp.float32) * s, 'b_qkv': jnp.zeros((3 * D_MODEL,), dtype=jnp.float32), 'w_gate': jax.random.normal(ks[2], (D_MODEL, D_MODEL), dtype=jnp.float32) * s, 'b_gate': jnp.zeros((D_MODEL,), dtype=jnp.float32), 'w_proj': jax.random.normal(ks[3], (D_MODEL, D_MODEL), dtype=jnp.float32) * s, 'b_proj': jnp.zeros((D_MODEL,), dtype=jnp.float32), 'ln_g': jnp.ones((D_MODEL,), dtype=jnp.float32), 'ln_b': jnp.zeros((D_MODEL,), dtype=jnp.float32)}
    _L0_attn_in = _L0_attn_setup()

    def _L0_ffn_setup():
        import jax, jax.numpy as jnp
        import numpy as np
        TOP_K = 2
        EPS = 1e-10
        key = jax.random.key(seed)
        k1, k2, k3, k4 = jax.random.split(key, 4)
        B, S, H, E = (4, 256, 128, 8)
        tokens = jax.random.normal(k1, (B, S, H), dtype=jnp.float32)
        router_w = jax.random.normal(k2, (E, H), dtype=jnp.float32) * (1.0 / np.sqrt(H))
        router_b = jax.random.normal(k3, (E,), dtype=jnp.float32) * 0.01
        expert_weights = jax.random.normal(k4, (E, H, H), dtype=jnp.float32) * (1.0 / np.sqrt(H))
        return {'tokens': tokens, 'router_w': router_w, 'router_b': router_b, 'expert_weights': expert_weights}
    _L0_ffn_in = _L0_ffn_setup()

    def _L1_attn_setup():
        import jax, jax.numpy as jnp
        import numpy as np
        D = 128
        HEADS = 16
        LN_EPS = 1e-05
        SHEP_EPS = 0.0001
        SHEP_P = 2

        def _shepards_mha(Q, K, V):
            q2 = jnp.sum(Q * Q, axis=-1, keepdims=True)
            k2 = jnp.sum(K * K, axis=-1, keepdims=True)
            sq = q2 + jnp.swapaxes(k2, -1, -2) - 2.0 * jnp.einsum('bhqd,bhkd->bhqk', Q, K)
            dist = jnp.sqrt(jnp.maximum(sq, 0.0))
            W = (SHEP_EPS + dist) ** (-SHEP_P)
            W = W / (SHEP_EPS + jnp.sum(W, axis=-1, keepdims=True))
            return jnp.einsum('bhqk,bhkd->bhqd', W, V)
        key = jax.random.key(seed)
        k1, k2, k3 = jax.random.split(key, 3)
        b, t, d = (2, 256, D)
        X = jax.random.normal(k1, (b, t, d), dtype=jnp.float32)
        W_in = jax.random.normal(k2, (4 * d, d), dtype=jnp.float32) * (1.0 / np.sqrt(d))
        b_in = jnp.zeros((4 * d,), dtype=jnp.float32)
        W_out = jax.random.normal(k3, (d, d), dtype=jnp.float32) * (1.0 / np.sqrt(d))
        b_out = jnp.zeros((d,), dtype=jnp.float32)
        return {'X': X, 'W_in': W_in, 'b_in': b_in, 'W_out': W_out, 'b_out': b_out}
    _L1_attn_in = _L1_attn_setup()

    def _L1_ffn_setup():
        import jax, jax.numpy as jnp
        import numpy as np
        E = 8
        TOPK = 2

        def _moe_forward(x, Wg, W1, W2, W3):
            B, S, D = x.shape
            xt = x.reshape(-1, D)
            T = xt.shape[0]
            logits = xt @ Wg.T
            scores = jax.nn.softmax(logits, axis=-1)
            w, idx = jax.lax.top_k(scores, TOPK)
            w = w / (w.sum(axis=-1, keepdims=True) + 1e-20)
            cw = jnp.zeros((T, E), xt.dtype).at[jnp.arange(T)[:, None], idx].add(w)
            h = jax.nn.silu(jnp.einsum('td,ehd->teh', xt, W1)) * jnp.einsum('td,ehd->teh', xt, W3)
            out = jnp.einsum('teh,edh->ted', h, W2)
            y = jnp.einsum('te,ted->td', cw, out)
            return y.reshape(B, S, D)
        key = jax.random.key(seed)
        k0, k1, k2, k3, k4 = jax.random.split(key, 5)
        B, S, D, H = (1, 256, 128, 352)
        scale = 0.02
        x = jax.random.normal(k0, (B, S, D), jnp.float32)
        Wg = jax.random.normal(k1, (E, D), jnp.float32) * scale
        W1 = jax.random.normal(k2, (E, H, D), jnp.float32) * scale
        W2 = jax.random.normal(k3, (E, D, H), jnp.float32) * scale
        W3 = jax.random.normal(k4, (E, H, D), jnp.float32) * scale
        return {'x': x, 'Wg': Wg, 'W1': W1, 'W2': W2, 'W3': W3}
    _L1_ffn_in = _L1_ffn_setup()
    _d = {'L0_attn_x': _L0_attn_in['x'], 'L0_attn_w_qkv': _L0_attn_in['w_qkv'], 'L0_attn_b_qkv': _L0_attn_in['b_qkv'], 'L0_attn_w_gate': _L0_attn_in['w_gate'], 'L0_attn_b_gate': _L0_attn_in['b_gate'], 'L0_attn_w_proj': _L0_attn_in['w_proj'], 'L0_attn_b_proj': _L0_attn_in['b_proj'], 'L0_attn_ln_g': _L0_attn_in['ln_g'], 'L0_attn_ln_b': _L0_attn_in['ln_b'], 'L0_ffn_router_w': _L0_ffn_in['router_w'], 'L0_ffn_router_b': _L0_ffn_in['router_b'], 'L0_ffn_expert_weights': _L0_ffn_in['expert_weights'], 'L1_attn_W_in': _L1_attn_in['W_in'], 'L1_attn_b_in': _L1_attn_in['b_in'], 'L1_attn_W_out': _L1_attn_in['W_out'], 'L1_attn_b_out': _L1_attn_in['b_out'], 'L1_ffn_Wg': _L1_ffn_in['Wg'], 'L1_ffn_W1': _L1_ffn_in['W1'], 'L1_ffn_W2': _L1_ffn_in['W2'], 'L1_ffn_W3': _L1_ffn_in['W3']}
    _x0 = _d['L0_attn_x']
    _d['L0_attn_x'] = jax.random.normal(jax.random.fold_in(jax.random.key(seed), 1), (8, 256, 128), dtype=_x0.dtype)
    del _x0
    return _d

def reference(L0_attn_x, L0_attn_w_qkv, L0_attn_b_qkv, L0_attn_w_gate, L0_attn_b_gate, L0_attn_w_proj, L0_attn_b_proj, L0_attn_ln_g, L0_attn_ln_b, L0_ffn_router_w, L0_ffn_router_b, L0_ffn_expert_weights, L1_attn_W_in, L1_attn_b_in, L1_attn_W_out, L1_attn_b_out, L1_ffn_Wg, L1_ffn_W1, L1_ffn_W2, L1_ffn_W3):

    def _L0_attn_ref(x, w_qkv, b_qkv, w_gate, b_gate, w_proj, b_proj, ln_g, ln_b):
        import jax, jax.numpy as jnp
        import numpy as np
        D_MODEL = 128
        B, T = (4, 512)
        LN_EPS = 1e-05
        DEN_EPS = 1e-06
        mu = jnp.mean(x, axis=-1, keepdims=True)
        var = jnp.mean(jnp.square(x - mu), axis=-1, keepdims=True)
        xn = (x - mu) * jax.lax.rsqrt(var + LN_EPS) * ln_g + ln_b
        qkv = xn @ w_qkv + b_qkv
        q, k, v = jnp.split(qkv, 3, axis=-1)
        gate = jax.nn.sigmoid(xn @ w_gate + b_gate)
        k = k * gate
        q = jax.nn.elu(q) + 1.0
        k = jax.nn.elu(k) + 1.0
        attn = jnp.einsum('btd,bsd->bts', q, k)
        tq = jnp.arange(q.shape[1])
        mask = (tq[:, None] >= tq[None, :]).astype(attn.dtype)
        attn = attn * mask
        out_num = jnp.einsum('bts,bsd->btd', attn, v)
        k_cumsum = jnp.cumsum(k, axis=1)
        out_den = jnp.sum(q * k_cumsum, axis=-1, keepdims=True) + DEN_EPS
        return out_num / out_den @ w_proj + b_proj

    def _L0_ffn_ref(tokens, router_w, router_b, expert_weights):
        import jax, jax.numpy as jnp
        import numpy as np
        TOP_K = 2
        EPS = 1e-10
        B, S, H = tokens.shape
        E = expert_weights.shape[0]
        logits = jnp.einsum('bsh,eh->bse', tokens, router_w) + router_b
        probs = jax.nn.softmax(logits, axis=-1)
        top_p, top_i = jax.lax.top_k(probs, TOP_K)
        w = top_p / (jnp.sum(top_p, axis=-1, keepdims=True) + EPS)
        x = tokens.reshape(-1, H)
        idx = top_i.reshape(-1, TOP_K)
        wf = w.reshape(-1, TOP_K)
        y_all = jnp.einsum('nh,ehd->ned', x, expert_weights)
        y_k = jnp.take_along_axis(y_all, idx[:, :, None], axis=1)
        out = jnp.einsum('nk,nkh->nh', wf, y_k)
        acc = jnp.clip(jnp.sum(wf, axis=-1), EPS, None)
        out = (out / acc[:, None]).reshape(B, S, H)
        scale = 1.0 + jnp.sum(w, axis=-1, keepdims=True) * EPS
        return out * scale

    def _L1_attn_ref(X, W_in, b_in, W_out, b_out):
        import jax, jax.numpy as jnp
        import numpy as np
        D = 128
        HEADS = 16
        LN_EPS = 1e-05
        SHEP_EPS = 0.0001
        SHEP_P = 2

        def _shepards_mha(Q, K, V):
            q2 = jnp.sum(Q * Q, axis=-1, keepdims=True)
            k2 = jnp.sum(K * K, axis=-1, keepdims=True)
            sq = q2 + jnp.swapaxes(k2, -1, -2) - 2.0 * jnp.einsum('bhqd,bhkd->bhqk', Q, K)
            dist = jnp.sqrt(jnp.maximum(sq, 0.0))
            W = (SHEP_EPS + dist) ** (-SHEP_P)
            W = W / (SHEP_EPS + jnp.sum(W, axis=-1, keepdims=True))
            return jnp.einsum('bhqk,bhkd->bhqd', W, V)
        b, t, d = X.shape
        h = HEADS
        dh = d // h
        mu = jnp.mean(X, axis=-1, keepdims=True)
        var = jnp.mean((X - mu) ** 2, axis=-1, keepdims=True)
        Xn = (X - mu) / jnp.sqrt(var + LN_EPS)
        P = jnp.einsum('btd,ed->bte', Xn, W_in) + b_in
        P = P.reshape(b, t, h, 4 * dh).transpose(0, 2, 1, 3)
        Q, K, V, G = jnp.split(P, 4, axis=-1)
        A = _shepards_mha(Q, K, V)
        O = (G * A).transpose(0, 2, 1, 3).reshape(b, t, d)
        return X + jnp.einsum('btd,ed->bte', O, W_out) + b_out

    def _L1_ffn_ref(x, Wg, W1, W2, W3):
        import jax, jax.numpy as jnp
        import numpy as np
        E = 8
        TOPK = 2

        def _moe_forward(x, Wg, W1, W2, W3):
            B, S, D = x.shape
            xt = x.reshape(-1, D)
            T = xt.shape[0]
            logits = xt @ Wg.T
            scores = jax.nn.softmax(logits, axis=-1)
            w, idx = jax.lax.top_k(scores, TOPK)
            w = w / (w.sum(axis=-1, keepdims=True) + 1e-20)
            cw = jnp.zeros((T, E), xt.dtype).at[jnp.arange(T)[:, None], idx].add(w)
            h = jax.nn.silu(jnp.einsum('td,ehd->teh', xt, W1)) * jnp.einsum('td,ehd->teh', xt, W3)
            out = jnp.einsum('teh,edh->ted', h, W2)
            y = jnp.einsum('te,ted->td', cw, out)
            return y.reshape(B, S, D)
        return _moe_forward(x, Wg, W1, W2, W3)
    x = L0_attn_x
    x = _layernorm(x + _L0_attn_ref(x, L0_attn_w_qkv, L0_attn_b_qkv, L0_attn_w_gate, L0_attn_b_gate, L0_attn_w_proj, L0_attn_b_proj, L0_attn_ln_g, L0_attn_ln_b), axis=-1)
    x = _layernorm(x + _L0_ffn_ref(x, L0_ffn_router_w, L0_ffn_router_b, L0_ffn_expert_weights), axis=-1)
    x = _layernorm(x + _L1_attn_ref(x, L1_attn_W_in, L1_attn_b_in, L1_attn_W_out, L1_attn_b_out), axis=-1)
    x = _layernorm(x + _L1_ffn_ref(x, L1_ffn_Wg, L1_ffn_W1, L1_ffn_W2, L1_ffn_W3), axis=-1)
    return x

_drawn_inputs = setup_inputs


def setup_inputs(seed=0):
    import zlib

    import numpy as np

    out = dict(_drawn_inputs(seed))
    spreads = {'L0_attn_b_qkv': (0.0, 0.1),
     'L0_attn_b_gate': (0.0, 2.0),
     'L0_attn_b_proj': (0.0, 0.1),
     'L0_attn_ln_g': (1.0, 0.2),
     'L0_attn_ln_b': (0.0, 0.1),
     'L1_attn_b_in': (0.0, 0.1),
     'L1_attn_b_out': (0.0, 0.1)}
    factors = {'L0_attn_w_gate': 5.034,
     'L1_ffn_Wg': 8.0,
     'L1_ffn_W1': 8.0,
     'L1_ffn_W2': 8.0,
     'L1_ffn_W3': 8.0}
    for name, (base, spread) in spreads.items():
        noise = np.random.default_rng([zlib.crc32(name.encode()), seed]).standard_normal(out[name].shape)
        drawn = base * np.exp(spread * noise) if base else spread * noise
        out[name] = jnp.asarray(drawn.astype(out[name].dtype))
    for name, factor in factors.items():
        out[name] = (out[name] * factor).astype(out[name].dtype)
    return out
```

```python
from contextlib import ExitStack

import concourse.bass as bass
from concourse import mybir

F32 = mybir.dt.float32
F32R = mybir.dt.float32r
ALU = mybir.AluOpType
ACT = mybir.ActivationFunctionType
AX = mybir.AxisListType.X

P = 128
SEQS, SEQ, D = 8, 256, 128
TOKENS = SEQS * SEQ
TILES = TOKENS // P
TPS = SEQ // P
E = 8
HEADS, DH = 16, 8
HW = 32
HG = P // HW
GROUPS = HEADS // HG
HID = 352
CHUNKS = [(0, 128), (128, 128), (256, 96)]
LN_EPS = 1e-5
DEN_EPS = 1e-6
TOPK_EPS = 1e-10
SHEP_EPS = 1e-4
MOE_EPS = 1e-20


def made(b, i=1, per=1):
    return (b + 2) * per + i


def freed(b, i=1, per=1):
    return b * per + i


def credit(eng, sem, per=1):
    eng.sem_inc(sem, 2 * per)


def landed(b, p, dmas=1):
    return (b - p) * (8 * dmas) + (16 * dmas + 1)


def after(eng, sem, value):
    if not isinstance(value, int) or value > 0:
        eng.wait_ge(sem, value)


def pipeline(eng, stages, n=SEQS, head=0):
    first = max(lag for lag, _ in stages) + head
    assert n > first and (n - first) % 2 == 0

    def irregular(i):
        for lag, stage in stages:
            if 0 <= i - lag < n:
                stage(i - lag, (i - lag) % 2)

    for i in range(first):
        irregular(i)
    with eng.Fori(0, (n - first) // 2) as pairs:
        for u in range(2):
            for lag, stage in stages:
                o = first + u - lag
                stage(pairs * 2 + o, o % 2)
    for i in range(n, n + first - head):
        irregular(i)


def idle(b, p):
    pass


def among_heads(of_head, others):
    listed = []
    for h in range(HEADS):
        stages = of_head(h)
        listed += (stages if isinstance(stages, list) else [stages]) + others.get(h, [])
    return listed


def tile_of(t, j):
    return bass.ds(t * TPS + j, 1)


def spread(ap, n):
    return ap.unsqueeze(len(ap.shape)).to_broadcast([*ap.shape, n])


class Kernel:

    def __init__(self, nc, ctx, dram, out):
        self.sem = lambda name: ctx.enter_context(nc.semaphore(name))
        self.settled = self.sem("settled")
        self.nc, self.dram, self.out = nc, dram, out
        sb = lambda name, shape, dt=F32: ctx.enter_context(nc.sbuf_tensor("sb_" + name, shape, dt))
        self.x = sb("x", [P, TILES, D])
        self.spare = sb("spare", [P, TILES, D])
        self.consts = sb("consts", [P, dram["consts"].shape[1]])
        self.ident = self.consts[:, 0:P]
        self.mask = self.consts[:, P:4 * P]
        self.index_rank = self.consts[:, 4 * P:5 * P]
        self.cols = sb("cols", [P, 8])
        self.rows = sb("rows", [P, dram["rows"].shape[1]])
        o = 0
        self.row = {}
        for name, n in ROWS:
            self.row[name] = self.rows[:, o:o + n]
            o += n
        self.w_qkvg = sb("w_qkvg", [P, 4 * D])
        self.w_proj = sb("w_proj", [P, D])
        self.w_router = sb("w_router", [P, 2, E])
        self.w_exp0 = sb("w_exp0", [P, E * D])
        self.w_in = sb("w_in", [P, 4 * D])
        self.w_out = sb("w_out", [P, D])
        self.loads = {"consts": self.consts, "cols": self.cols, "rows": self.rows, "w_qkvg": self.w_qkvg,
                      "w_proj": self.w_proj, "w_router": self.w_router, "w_exp0": self.w_exp0, "w_in": self.w_in,
                      "w_out": self.w_out}
        self.logits = sb("logits", [P, TILES, E])
        self.cw = sb("cw", [P, TILES, E])
        self.cw_by_expert = sb("cw_by_expert", [P, E, TILES])
        self.x_high, self.x_low = sb("x_high", [P, TOKENS], F32R), sb("x_low", [P, TOKENS], F32R)
        self.yT = sb("yT", [P, TOKENS])
        self.minus_half = sb("minus_half", [P, TPS])
        self.psum = [ctx.enter_context(nc.psum_tensor(f"bank{i}", [P, 512], F32)) for i in range(8)]


    def settle(self, eng):
        eng.sem_inc(self.settled, 1)


ROWS = [("b_v", TPS * D), ("b_proj", D), ("b_router", TILES * E), ("b_in", 4 * D), ("b_out", D)]


def layer0_attention(k):
    nc = k.nc
    with ExitStack() as c:
        sb = lambda name, shape: c.enter_context(nc.sbuf_tensor("a_" + name, shape, F32))
        pair = lambda name, shape: [sb(f"{name}{i}", shape) for i in range(2)]
        stats, mv, rstd = pair("stats", [P, TPS, 6]), pair("mv", [P, TPS, 2]), pair("rstd", [P, TPS])
        xn, xnT = pair("xn", [P, TPS, D]), pair("xnT", [P, SEQ])
        qk, low, features = (pair(name, [P, 2 * SEQ]) for name in ("qk", "low", "features"))
        v, th = pair("v", [P, TPS, D]), pair("th", [P, SEQ])
        attn, numT, rden = pair("attn", [P, 3 * P]), pair("numT", [P, SEQ]), pair("rden", [P, TPS])
        xb = pair("xb", [P, TPS, D])
        stats1, mv1, rstd1 = pair("stats1", [P, TPS, 6]), pair("mv1", [P, TPS, 2]), pair("rstd1", [P, TPS])
        x1T, x1 = pair("x1T", [P, SEQ]), pair("x1", [P, TPS, D])
        ones = sb("ones", [P, 1])
        t_bank, qk_bank, gate_bank, attn_bank, num_bank, x1_bank, v_bank, proj_bank = k.psum

        s_first, s_x, s_now, s_w = (k.sem("a_" + name) for name in ("x_first", "x_in", "w_now", "w_in"))
        s_set = k.sem("a_set")
        names = ("stats moments var rstd xn xnT_p xnT gate_p qk_p v_p th q kb v kg low exp features attn_p attn num_p numT "
                 "rden0 rden proj_p xb r stats1 moments1 var1 rstd1 x1 kept x1T_p x1T logits_p logits").split()
        s = {n: k.sem("a_" + n) for n in names}
        block = c.enter_context(nc.Block())
        NOW = "cols w_qkvg consts rows".split()
        LATER = "w_proj w_router w_exp0 w_in w_out".split()

        @block.sync
        def _(sp):
            x_in = k.dram["x"].rearrange("b (j p) d -> p (b j) d", p=P)
            sp.dma_start(k.x[:, 0:TPS, :], x_in[:, 0:TPS, :]).then_inc(s_first, 16)
            sp.dma_start(k.consts[:], k.dram["consts"]).then_inc(s_now, 16)
            for b in range(1, SEQS):
                sp.dma_start(k.x[:, TPS * b:TPS * b + TPS, :], x_in[:, TPS * b:TPS * b + TPS, :]).then_inc(s_x, 16)

        @block.scalar
        def _(act):
            for name in NOW:
                if name != "consts":
                    act.dma_start(k.loads[name][:], k.dram[name]).then_inc(s_now, 16)
            for name in LATER:
                act.dma_start(k.loads[name][:], k.dram[name]).then_inc(s_w, 16)
            for name in ("xnT", "th", "exp", "numT", "x1T"):
                credit(act, s[name])
            act.wait_ge(s_now, 16 * len(NOW))
            act.wait_ge(s_set, 3)

            def norm_t(b, p):
                act.wait_ge(s["xnT_p"], made(b))
                after(act, s["v_p"], freed(b))
                nc.scalar.activation(xnT[p][:], t_bank[:, 0:SEQ], ACT.Identity, scale=k.cols[:, 3:4],
                                     bias=k.cols[:, 4:5]).then_inc(s["xnT"], 1)

            def gate(b, p):
                act.wait_ge(s["gate_p"], made(b))
                after(act, s["kg"], freed(b))
                nc.scalar.activation(th[p][:], gate_bank[:, 0:SEQ], ACT.Tanh, scale=0.5,
                                     bias=k.cols[:, 5:6]).then_inc(s["th"], 1)

            def exponentials(b, p):
                act.wait_ge(s["low"], made(b))
                nc.scalar.activation(low[p][:], low[p][:], ACT.Exp).then_inc(s["exp"], 1)

            def numerators(b, p):
                act.wait_ge(s["num_p"], made(b))
                after(act, s["proj_p"], freed(b))
                nc.scalar.activation(numT[p][:], num_bank[:, 0:SEQ], ACT.Copy).then_inc(s["numT"], 1)

            def turned(b, p):
                act.wait_ge(s["x1T_p"], made(b))
                after(act, s["logits_p"], freed(b))
                nc.scalar.activation(x1T[p][:], x1_bank[:, 0:SEQ], ACT.Copy).then_inc(s["x1T"], 1)

            pipeline(act, [(3, exponentials), (6, turned), (1, norm_t), (4, numerators), (2, gate)])

        @block.gpsimd
        def _(pool):
            for name in ("var", "rstd", "xb", "var1", "rstd1", "kept"):
                credit(pool, s[name])
            pool.memset(k.minus_half[:], -0.5).then_inc(s_set, 1)
            pool.memset(ones[:], 1.0).then_inc(s_set, 1)
            pool.wait_ge(s_set, 2)
            pool.wait_ge(s_now, 16 * len(NOW))

            def norm(b, p):
                pool.wait_ge(s["moments"], made(b))
                rstd_of(k, pool, b, rstd[p], mv[p], s["var"]).then_inc(s["rstd"], 1)

            def residual(b, p):
                pool.wait_ge(s["stats"], made(b))
                after(pool, s["r"], freed(b))
                for j in range(TPS):
                    last = pool.tensor_tensor(xb[p][:, j:j + 1, :], k.x[:, tile_of(b, j), :], k.row["b_proj"].unsqueeze(1), ALU.add)
                last.then_inc(s["xb"], 1)

            def norm1(b, p):
                pool.wait_ge(s["moments1"], made(b))
                rstd_of(k, pool, b, rstd1[p], mv1[p], s["var1"]).then_inc(s["rstd1"], 1)

            def keep(b, p):
                pool.wait_ge(s["x1"], made(b))
                k.settle(pool)
                pool.tensor_copy(k.x[:, bass.ds(b * TPS, TPS), :], x1[p][:]).then_inc(s["kept"], 1)

            pipeline(pool, [(6, keep), (4, residual), (5, norm1), (0, norm)])

        @block.vector
        def _(dve):
            for name in ("stats moments xn q kb v kg low features attn rden0 rden r stats1 moments1 x1 logits").split():
                credit(dve, s[name])
            dve.wait_ge(s_now, 16 * len(NOW))
            nc.vector.tensor_scalar(k.cols[:, 5:6], k.cols[:, 2:3], 0.5, None, ALU.mult).then_inc(s_set, 1)
            dve.wait_ge(s_first, 16)

            def norm_a(b, p):
                if not isinstance(b, int) or b > 0:
                    dve.wait_ge(s_x, 16 * (SEQS - 1))
                statistics(k, dve, lambda j: k.x[:, tile_of(b, j), :], stats[p]).then_inc(s["stats"], 1)

            def norm_b(b, p):
                dve.wait_ge(s["stats"], made(b))
                moments(k, dve, stats[p], mv[p]).then_inc(s["moments"], 1)

            def norm_x(b, p):
                dve.wait_ge(s["rstd"], made(b))
                after(dve, s["xnT_p"], freed(b))
                for j in range(TPS):
                    last = normalise(nc, xn[p][:, j:j + 1, :], k.x[:, tile_of(b, j), :], mv[p], rstd[p], j)
                last.then_inc(s["xn"], 1)

            def project(b, p):
                dve.wait_ge(s["qk_p"], made(b))
                nc.vector.tensor_scalar(qk[p][:, 0:SEQ], qk_bank[:, 0:SEQ], k.cols[:, 0:1], None, ALU.add).then_inc(s["q"], 1)
                nc.vector.tensor_scalar(qk[p][:, SEQ:2 * SEQ], qk_bank[:, SEQ:2 * SEQ], k.cols[:, 1:2], 0.5, ALU.add,
                                        ALU.mult).then_inc(s["kb"], 1)

            def values(b, p):
                dve.wait_ge(s["v_p"], made(b))
                after(dve, s["num_p"], freed(b))
                nc.vector.tensor_tensor(v[p][:], v_bank[:, 0:SEQ].rearrange("p (j d) -> p j d", j=TPS),
                                        k.row["b_v"].rearrange("p (j d) -> p j d", j=TPS), ALU.add).then_inc(s["v"], 1)

            def gate(b, p):
                dve.wait_ge(s["th"], made(b))
                dve.wait_ge(s["kb"], made(b))
                keys = qk[p][:, SEQ:2 * SEQ]
                nc.vector.scalar_tensor_tensor(keys, th[p][:], 1.0, keys, ALU.add, ALU.mult).then_inc(s["kg"], 1)

            def lows(b, p):
                dve.wait_ge(s["q"], made(b))
                dve.wait_ge(s["kg"], made(b))
                nc.vector.tensor_scalar(low[p][:], qk[p][:], 0.0, None, ALU.min).then_inc(s["low"], 1)

            def features_of(b, p):
                dve.wait_ge(s["exp"], made(b))
                after(dve, s["attn_p"], freed(b))
                nc.vector.scalar_tensor_tensor(features[p][:], qk[p][:], 1.0, low[p][:], ALU.add, ALU.max
                                               ).then_inc(s["features"], 1)

            def mask(b, p):
                dve.wait_ge(s["attn_p"], made(b))
                after(dve, s["num_p"], freed(b))
                nc.vector.tensor_tensor(attn[p][:], attn_bank[:, 0:3 * P], k.mask, ALU.mult).then_inc(s["attn"], 1)

            def denominators(b, p):
                dve.wait_ge(s["numT"], made(b))
                nc.vector.tensor_scalar(rden[p][:], num_bank[:, SEQ:SEQ + TPS], DEN_EPS, None, ALU.add).then_inc(s["rden0"], 1)

            def inverses(b, p):
                dve.wait_ge(s["rden0"], made(b))
                nc.vector.reciprocal(rden[p][:], rden[p][:]).then_inc(s["rden"], 1)

            def add(b, p):
                dve.wait_ge(s["proj_p"], made(b))
                dve.wait_ge(s["rden"], made(b))
                dve.wait_ge(s["xb"], made(b))
                for j in range(TPS):
                    last = nc.vector.scalar_tensor_tensor(k.spare[:, tile_of(b, j), :], proj_bank[:, j * D:(j + 1) * D].unsqueeze(1),
                                                          rden[p][:, j:j + 1], xb[p][:, j:j + 1, :], ALU.mult, ALU.add)
                last.then_inc(s["r"], 1)

            def norm1_a(b, p):
                dve.wait_ge(s["r"], made(b))
                statistics(k, dve, lambda j: k.spare[:, tile_of(b, j), :], stats1[p]).then_inc(s["stats1"], 1)

            def norm1_b(b, p):
                dve.wait_ge(s["stats1"], made(b))
                moments(k, dve, stats1[p], mv1[p]).then_inc(s["moments1"], 1)

            def norm1_x(b, p):
                dve.wait_ge(s["rstd1"], made(b))
                after(dve, s["x1T_p"], freed(b))
                after(dve, s["kept"], freed(b))
                for j in range(TPS):
                    last = normalise(nc, x1[p][:, j:j + 1, :], k.spare[:, tile_of(b, j), :], mv1[p], rstd1[p], j)
                last.then_inc(s["x1"], 1)

            def logits(b, p):
                dve.wait_ge(s["logits_p"], made(b))
                nc.vector.tensor_tensor(k.logits[:, bass.ds(b * TPS, TPS), :],
                                        x1_bank[:, SEQ:SEQ + TPS * E].rearrange("p (j e) -> p j e", j=TPS),
                                        k.row["b_router"][:, 0:TPS * E].rearrange("p (j e) -> p j e", j=TPS),
                                        ALU.add).then_inc(s["logits"], 1)

            pipeline(dve, [(6, norm1_x), (1, norm_x), (4, mask), (0, norm_a), (5, add), (3, features_of), (0, norm_b),
                           (5, norm1_a), (2, project), (5, norm1_b), (2, values), (2, gate), (4, denominators), (2, lows),
                           (4, inverses), (6, logits)])

        @block.tensor
        def _(pe):
            for name in "xnT_p qk_p gate_p v_p attn_p num_p proj_p x1T_p logits_p".split():
                credit(pe, s[name])
            pe.wait_ge(s_now, 16 * len(NOW))
            pe.wait_ge(s_set, 3)

            def norm_t(b, p):
                pe.wait_ge(s["xn"], made(b))
                pe.wait_ge(s["xnT"], made(b - 1))
                for j in range(TPS):
                    last = nc.tensor.transpose(t_bank[:, j * P:(j + 1) * P], xn[p][:, j, :], k.ident)
                last.then_inc(s["xnT_p"], 1)

            def project(b, p):
                pe.wait_ge(s["xnT"], made(b))
                pe.wait_ge(s["th"], made(b - 1))
                nc.tensor.matmul(gate_bank[:, 0:SEQ], k.w_qkvg[:, 3 * D:4 * D], xnT[p][:], start=True, stop=True
                                 ).then_inc(s["gate_p"], 1)
                pe.wait_ge(s["kb"], made(b - 1))
                nc.tensor.matmul(qk_bank[:, 0:SEQ], k.w_qkvg[:, 0:D], xnT[p][:], start=True, stop=True)
                nc.tensor.matmul(qk_bank[:, SEQ:2 * SEQ], k.w_qkvg[:, D:2 * D], xnT[p][:], start=True, stop=True
                                 ).then_inc(s["qk_p"], 1)
                pe.wait_ge(s["v"], made(b - 1))
                for j in range(TPS):
                    last = nc.tensor.matmul(v_bank[:, j * D:(j + 1) * D], xnT[p][:, j * P:(j + 1) * P],
                                            k.w_qkvg[:, 2 * D:3 * D], start=True, stop=True)
                last.then_inc(s["v_p"], 1)

            def attend(b, p):
                pe.wait_ge(s["features"], made(b))
                pe.wait_ge(s["attn"], made(b - 1))
                f = features[p]
                nc.tensor.matmul(attn_bank[:, 0:SEQ], f[:, SEQ:SEQ + P], f[:, 0:SEQ], start=True, stop=True)
                nc.tensor.matmul(attn_bank[:, SEQ:SEQ + P], f[:, SEQ + P:2 * SEQ], f[:, P:SEQ], start=True, stop=True
                                 ).then_inc(s["attn_p"], 1)

            def apply(b, p):
                pe.wait_ge(s["attn"], made(b))
                pe.wait_ge(s["v"], made(b))
                pe.wait_ge(s["rden0"], made(b - 1))
                nc.tensor.matmul(num_bank[:, 0:P], v[p][:, 0, :], attn[p][:, 0:P], start=True, stop=True)
                nc.tensor.matmul(num_bank[:, P:SEQ], v[p][:, 0, :], attn[p][:, P:SEQ], start=True, stop=False)
                nc.tensor.matmul(num_bank[:, P:SEQ], v[p][:, 1, :], attn[p][:, SEQ:SEQ + P], start=False, stop=True)
                nc.tensor.matmul(num_bank[:, SEQ:SEQ + 1], attn[p][:, 0:P], ones[:], start=True, stop=True)
                nc.tensor.matmul(num_bank[:, SEQ + 1:SEQ + 2], attn[p][:, P:SEQ], ones[:], start=True, stop=False)
                nc.tensor.matmul(num_bank[:, SEQ + 1:SEQ + 2], attn[p][:, SEQ:SEQ + P], ones[:], start=False, stop=True
                                 ).then_inc(s["num_p"], 1)

            def out(b, p):
                pe.wait_ge(s["numT"], made(b))
                pe.wait_ge(s["r"], made(b - 1))
                if isinstance(b, int) and b == 0:
                    pe.wait_ge(s_w, 16 * len(LATER))
                for j in range(TPS):
                    last = nc.tensor.matmul(proj_bank[:, j * D:(j + 1) * D], numT[p][:, j * P:(j + 1) * P], k.w_proj[:],
                                            start=True, stop=True)
                last.then_inc(s["proj_p"], 1)

            def turn(b, p):
                pe.wait_ge(s["x1"], made(b))
                pe.wait_ge(s["logits"], made(b - 1))
                for j in range(TPS):
                    last = nc.tensor.transpose(x1_bank[:, j * P:(j + 1) * P], x1[p][:, j, :], k.ident)
                last.then_inc(s["x1T_p"], 1)

            def logits(b, p):
                pe.wait_ge(s["x1T"], made(b))
                for j in range(TPS):
                    last = nc.tensor.matmul(x1_bank[:, SEQ + j * E:SEQ + (j + 1) * E], x1T[p][:, j * P:(j + 1) * P],
                                            k.w_router[:, 0, :], start=True, stop=True)
                last.then_inc(s["logits_p"], 1)

            pipeline(pe, [(5, out), (2, project), (6, turn), (1, norm_t), (4, apply), (3, attend), (6, logits)])


def router(k, c, layer):
    nc = k.nc
    full = [c.enter_context(nc.sbuf_tensor(f"rt{layer}_{i}", [P, TILES, E], F32)) for i in range(6)]
    few = [c.enter_context(nc.sbuf_tensor(f"rf{layer}_{i}", [P, TILES], F32)) for i in range(8)]
    shifted, probs, picked, equal, rest, second = full
    top, total, best, next_best, place, w1, w2, scale = few
    s_step, s_shifted, s_exp, s_routed = (k.sem(f"rt_{name}{layer}") for name in "step shifted exp routed".split())
    rank = k.index_rank.rearrange("p (t e) -> p t e", t=TILES)

    def on_scalar(act):
        act.wait_ge(s_shifted, 1)
        nc.scalar.activation(probs[:], shifted[:], ACT.Exp).then_inc(s_exp, 1)

    def on_vector(dve):
        steps = [0]

        def step(instruction):
            steps[0] += 1
            instruction.then_inc(s_step, 1)
            dve.wait_ge(s_step, steps[0])

        def largest(out, values):
            step(nc.vector.tensor_reduce(out[:], values[:], AX, ALU.max))

        def first_at(out, values, value):
            step(nc.vector.tensor_tensor(out[:], values[:], spread(value[:], E), ALU.is_equal))
            step(nc.vector.tensor_tensor(out[:], out[:], rank, ALU.mult))
            largest(place, out)
            step(nc.vector.tensor_tensor(out[:], out[:], spread(place[:], E), ALU.is_equal))

        largest(top, k.logits)
        nc.vector.tensor_tensor(shifted[:], k.logits[:], spread(top[:], E), ALU.subtract).then_inc(s_shifted, 1)
        dve.wait_ge(s_exp, 1)
        step(nc.vector.tensor_reduce(total[:], probs[:], AX, ALU.add))
        step(nc.vector.reciprocal(total[:], total[:]))
        step(nc.vector.tensor_tensor(probs[:], probs[:], spread(total[:], E), ALU.mult))
        largest(best, probs)
        first_at(picked, probs, best)
        step(nc.vector.scalar_tensor_tensor(rest[:], picked[:], -2.0, probs[:], ALU.mult, ALU.add))
        largest(next_best, rest)
        first_at(second, rest, next_best)
        step(nc.vector.tensor_tensor(picked[:], picked[:], second[:], ALU.add))
        step(nc.vector.tensor_tensor(picked[:], picked[:], probs[:], ALU.mult))
        step(nc.vector.tensor_tensor(scale[:], best[:], next_best[:], ALU.add))
        step(nc.vector.tensor_scalar(scale[:], scale[:], MOE_EPS if layer else TOPK_EPS, None, ALU.add))
        step(nc.vector.reciprocal(scale[:], scale[:]))
        if layer == 0:
            step(nc.vector.tensor_tensor(w1[:], best[:], scale[:], ALU.mult))
            step(nc.vector.tensor_tensor(w2[:], next_best[:], scale[:], ALU.mult))
            step(nc.vector.tensor_tensor(w1[:], w1[:], w2[:], ALU.add))
            step(nc.vector.tensor_scalar(w2[:], w1[:], TOPK_EPS, None, ALU.max))
            step(nc.vector.reciprocal(w2[:], w2[:]))
            step(nc.vector.tensor_scalar(w1[:], w1[:], TOPK_EPS, 1.0, ALU.mult, ALU.add))
            step(nc.vector.tensor_tensor(w1[:], w1[:], w2[:], ALU.mult))
            step(nc.vector.tensor_tensor(scale[:], scale[:], w1[:], ALU.mult))
        out = k.cw_by_expert[:].rearrange("p e t -> p t e") if layer else k.cw[:]
        nc.vector.tensor_tensor(out, picked[:], spread(scale[:], E), ALU.mult).then_inc(s_routed, 1)

    return on_scalar, on_vector, s_routed


def layer0_experts(k):
    nc = k.nc
    with ExitStack() as c:
        sb = lambda name, shape: c.enter_context(nc.sbuf_tensor("e_" + name, shape, F32))
        pair = lambda name, shape: [sb(f"{name}{i}", shape) for i in range(2)]
        HALF = E // 2
        xc, xT = pair("xc", [P, TPS, D]), pair("xT", [P, SEQ])
        wy = pair("wy", [P, TPS, 2, HALF * D])
        quad, duo, one = pair("quad", [P, TPS, 4 * D]), pair("duo", [P, TPS, 2 * D]), pair("one", [P, TPS, D])
        r = pair("r", [P, TPS, D])
        stats, mv, rstd = pair("stats", [P, TPS, 6]), pair("mv", [P, TPS, 2]), pair("rstd", [P, TPS])
        t_bank, y_banks = k.psum[7], k.psum[0:4]
        names = "xc xT_p xT y_p wy_act wy_dve quad duo one r stats moments var rstd x2".split()
        s = {n: k.sem("e_" + n) for n in names}
        per = dict(y_p=TPS, wy_act=TPS, wy_dve=TPS)
        route_on_scalar, route_on_vector, s_routed = router(k, c, 0)
        block = c.enter_context(nc.Block(no_gpsimd_drain=True))

        @block.gpsimd
        def _(pool):
            for name in "xc duo one var rstd".split():
                credit(pool, s[name])

            def fetch(b, p):
                after(pool, s["xT_p"], freed(b))
                k.settle(pool)
                pool.tensor_copy(xc[p][:], k.x[:, bass.ds(b * TPS, TPS), :]).then_inc(s["xc"], 1)

            def add(b, p):
                pool.wait_ge(s["quad"], made(b))
                pool.tensor_tensor(duo[p][:], quad[p][:, :, 0:2 * D], quad[p][:, :, 2 * D:4 * D], ALU.add).then_inc(s["duo"], 1)
                pool.wait_ge(s["duo"], made(b))
                after(pool, s["r"], freed(b))
                pool.tensor_tensor(one[p][:], duo[p][:, :, 0:D], duo[p][:, :, D:2 * D], ALU.add).then_inc(s["one"], 1)

            def norm(b, p):
                pool.wait_ge(s["moments"], made(b))
                rstd_of(k, pool, b, rstd[p], mv[p], s["var"]).then_inc(s["rstd"], 1)

            pipeline(pool, [(0, fetch), (2, add), (3, norm), (4, idle)])

        @block.scalar
        def _(act):
            for name in ("xT", "wy_act"):
                credit(act, s[name], per.get(name, 1))
            route_on_scalar(act)

            def turned(b, p):
                act.wait_ge(s["xT_p"], made(b))
                after(act, s["y_p"], freed(b, TPS, TPS))
                nc.scalar.activation(xT[p][:], t_bank[:, 0:SEQ], ACT.Copy).then_inc(s["xT"], 1)

            def weigh(b, p):
                if isinstance(b, int) and b == 0:
                    act.wait_ge(s_routed, 1)
                after(act, s["quad"], freed(b))
                for j in range(TPS):
                    act.wait_ge(s["y_p"], made(b, j + 1, TPS))
                    for e in range(HALF):
                        k.settle(act)
                        last = nc.scalar.activation(
                            wy[p][:, j, 0, e * D:(e + 1) * D].unsqueeze(1), y_banks[2 * j][:, e * D:(e + 1) * D].unsqueeze(1),
                            ACT.Copy, scale=k.cw[:, tile_of(b, j), e])
                    last.then_inc(s["wy_act"], 1)

            pipeline(act, [(1, weigh), (0, turned), (4, idle)])

        @block.vector
        def _(dve):
            for name in "wy_dve quad r stats moments x2".split():
                credit(dve, s[name], per.get(name, 1))
            route_on_vector(dve)
            dve.wait_ge(s_routed, 1)

            def weigh(j):
                def stage(b, p):
                    after(dve, s["quad"], freed(b))
                    dve.wait_ge(s["y_p"], made(b, j + 1, TPS))
                    w = k.cw[:, tile_of(b, j), HALF:E].rearrange("p t e -> p (t e)")
                    nc.vector.tensor_tensor(wy[p][:, j, 1].rearrange("p (e d) -> p e d", d=D),
                                            y_banks[2 * j + 1][:].rearrange("p (e d) -> p e d", d=D), spread(w, D), ALU.mult
                                            ).then_inc(s["wy_dve"], 1)
                return stage

            def add(b, p):
                dve.wait_ge(s["wy_act"], made(b, TPS, TPS))
                dve.wait_ge(s["wy_dve"], made(b, TPS, TPS))
                after(dve, s["duo"], freed(b))
                nc.vector.tensor_tensor(quad[p][:], wy[p][:, :, 0], wy[p][:, :, 1], ALU.add).then_inc(s["quad"], 1)

            def residual(b, p):
                dve.wait_ge(s["one"], made(b))
                k.settle(dve)
                nc.vector.tensor_tensor(r[p][:], k.x[:, bass.ds(b * TPS, TPS), :], one[p][:], ALU.add).then_inc(s["r"], 1)

            def norm_a(b, p):
                dve.wait_ge(s["r"], made(b))
                statistics(k, dve, lambda j: r[p][:, j, :], stats[p]).then_inc(s["stats"], 1)

            def norm_b(b, p):
                dve.wait_ge(s["stats"], made(b))
                moments(k, dve, stats[p], mv[p]).then_inc(s["moments"], 1)

            def norm_x(b, p):
                dve.wait_ge(s["rstd"], made(b))
                for j in range(TPS):
                    last = normalise(nc, k.x[:, tile_of(b, j), :], r[p][:, j:j + 1, :], mv[p], rstd[p], j)
                last.then_inc(s["x2"], 1)

            pipeline(dve, [(4, norm_x), (2, add), (3, residual), (1, weigh(0)), (3, norm_a), (1, weigh(1)), (3, norm_b)])

        @block.tensor
        def _(pe):
            for name in ("xT_p", "y_p"):
                credit(pe, s[name], per.get(name, 1))

            def turn(b, p):
                pe.wait_ge(s["xc"], made(b))
                pe.wait_ge(s["xT"], made(b - 1))
                for j in range(TPS):
                    last = nc.tensor.transpose(t_bank[:, j * P:(j + 1) * P], xc[p][:, j, :], k.ident)
                last.then_inc(s["xT_p"], 1)

            def experts(b, p):
                pe.wait_ge(s["xT"], made(b))
                for j in range(TPS):
                    pe.wait_ge(s["wy_act"], made(b - 1, j + 1, TPS))
                    pe.wait_ge(s["wy_dve"], made(b - 1, j + 1, TPS))
                    for h in range(2):
                        last = nc.tensor.matmul(y_banks[2 * j + h][:], xT[p][:, j * P:(j + 1) * P],
                                                k.w_exp0[:, h * 4 * D:(h + 1) * 4 * D], start=True, stop=True)
                    last.then_inc(s["y_p"], 1)

            pipeline(pe, [(1, experts), (0, turn), (4, idle)])


def statistics(k, dve, rows, st):
    k.settle(dve)
    for j in range(TPS):
        last = k.nc.vector.bn_stats(st[:, j, :], rows(j))
    return last


def moments(k, dve, st, m):
    k.settle(dve)
    for j in range(TPS):
        last = k.nc.vector.bn_aggr(m[:, j, :], st[:, j, :])
    return last


def rstd_of(k, pool, b, rs, m, s_var):
    k.settle(pool)
    pool.tensor_scalar(rs[:], m[:, :, 1], LN_EPS, None, ALU.add).then_inc(s_var, 1)
    pool.wait_ge(s_var, made(b))
    return pool.tensor_tensor(rs[:], rs[:], k.minus_half[:], ALU.pow)


def normalise(nc, dst, src, m, rs, j):
    return nc.vector.tensor_scalar(dst, src, m[:, j, 0:1], rs[:, j:j + 1], ALU.subtract, ALU.mult)


def layer1_attention(k):
    nc = k.nc
    QUERY, KEY = 0, 1
    Q_NORM, K_NORM, USED = 3 * DH + 2, 3 * DH, 3 * DH + 4
    PART = 4
    PARTS = HEADS // PART
    D_BANKS = 3
    FILLS = 4
    with ExitStack() as c:
        sb = lambda name, shape, dt=F32: c.enter_context(nc.sbuf_tensor("s_" + name, shape, dt))
        pair = lambda name, shape, dt=F32: [sb(f"{name}{i}", shape, dt) for i in range(2)]
        stats, mv, rstd = pair("stats", [P, TPS, 6]), pair("mv", [P, TPS, 2]), pair("rstd", [P, TPS])
        xn, xnT = pair("xn", [P, TPS, D]), pair("xnT", [P, SEQ])
        qk = pair("qk", [P, TPS, 2, HEADS, DH])
        squares, norms = pair("squares", [P, TPS, 2, HEADS, DH]), pair("norms", [P, TPS, 2, HEADS])
        slots = pair("slots", [P, TPS, 2, HEADS, HW])
        slotsT = pair("slotsT", [P, 2 * GROUPS, TPS, P], F32R)
        values_all, gates = sb("values_all", [P, TILES, HEADS, DH]), k.spare
        values = pair("values", [P, TPS, HEADS, HW])
        w = pair("w", [P, HEADS, TPS * SEQ])
        avT = pair("avT", [P, GROUPS, SEQ])
        rden = pair("rden", [P, TPS, HEADS])
        o, xb, r = (pair(n, [P, TPS, D]) for n in ("o", "xb", "r"))
        oT = pair("oT", [P, SEQ])
        stats1, mv1, rstd1 = pair("stats1", [P, TPS, 6]), pair("mv1", [P, TPS, 2]), pair("rstd1", [P, TPS])
        x3, x3T = pair("x3", [P, TPS, D]), pair("x3T", [P, SEQ])
        eps = sb("eps", [P, 1])
        t_bank, p_bank, d_banks, avT_banks, out_bank = k.psum[0], k.psum[1], k.psum[2:5], k.psum[5:7], k.psum[7]
        av_banks = avT_banks[1], t_bank
        names = ("stats moments var rstd xn xnT_p xnT p_p qkvg high lows squares norms norms_high slots slots_p slotsT "
                 "d_p d dist logd w values avT_p avT av_p rden0 rden o0 o oT_p oT out_p xb0 xb r "
                 "stats1 moments1 var1 rstd1 x3 kept x3T_p x3T logits_p logits x_high x_low").split()
        s = {n: k.sem("h_" + n) for n in names}
        per = dict(p_p=TPS, qkvg=TPS, slots_p=FILLS, slotsT=FILLS, d_p=HEADS, d=HEADS, dist=PARTS, logd=PARTS,
                   w=PARTS, avT_p=2, avT=2)
        s_set = k.sem("h_set")
        block = c.enter_context(nc.Block(no_gpsimd_drain=True))

        @block.gpsimd
        def _(pool):
            for name in "var rstd squares lows values xb0 xb o var1 rstd1 kept x_high x_low".split():
                credit(pool, s[name])
            pool.memset(eps[:], SHEP_EPS).then_inc(s_set, 1)
            for t in slots:
                pool.memset(t[:], -0.5).then_inc(s_set, 1)
            for t in values:
                pool.memset(t[:], 1.0).then_inc(s_set, 1)
            pool.wait_ge(s_set, 5)

            def norm(b, p):
                pool.wait_ge(s["moments"], made(b))
                rstd_of(k, pool, b, rstd[p], mv[p], s["var"]).then_inc(s["rstd"], 1)

            def square(b, p):
                pool.wait_ge(s["qkvg"], made(b, TPS, TPS))
                after(pool, s["norms"], freed(b))
                pool.tensor_tensor(squares[p][:], qk[p][:], qk[p][:], ALU.mult).then_inc(s["squares"], 1)

            def lows(b, p):
                pool.wait_ge(s["high"], made(b))
                for q, at in ((QUERY, 2 * DH), (KEY, DH)):
                    last = pool.tensor_tensor(slots[p][:, :, q, :, at:at + DH], qk[p][:, :, q], slots[p][:, :, q, :, 0:DH],
                                              ALU.subtract)
                last.then_inc(s["lows"], 1)

            def place_values(b, p):
                after(pool, s["avT_p"], freed(b, 2, 2))
                k.settle(pool)
                pool.tensor_copy(values[p][:, :, :, 0:DH], values_all[:, bass.ds(b * TPS, TPS), :, :]).then_inc(s["values"], 1)

            def gate(b, p):
                pool.wait_ge(s["o0"], made(b))
                k.settle(pool)
                pool.tensor_tensor(o[p][:], o[p][:], gates[:, bass.ds(b * TPS, TPS), :], ALU.mult).then_inc(s["o"], 1)

            def residual(b, p):
                after(pool, s["r"], freed(b))
                k.settle(pool)
                for j in range(TPS):
                    last = pool.tensor_tensor(xb[p][:, j:j + 1, :], k.x[:, tile_of(b, j), :],
                                              k.row["b_out"].unsqueeze(1), ALU.add)
                last.then_inc(s["xb0"], 1)
                pool.wait_ge(s["xb0"], made(b))
                k.settle(pool)
                pool.tensor_tensor(xb[p][:], k.x[:, bass.ds(b * TPS, TPS), :], xb[p][:], ALU.add).then_inc(s["xb"], 1)

            def norm1(b, p):
                pool.wait_ge(s["moments1"], made(b))
                rstd_of(k, pool, b, rstd1[p], mv1[p], s["var1"]).then_inc(s["rstd1"], 1)

            def keep(b, p):
                pool.wait_ge(s["x3"], made(b))
                k.settle(pool)
                pool.tensor_copy(k.x[:, bass.ds(b * TPS, TPS), :], x3[p][:]).then_inc(s["kept"], 1)

            def split(b, p):
                pool.wait_ge(s["x3T"], made(b))
                k.settle(pool)
                cols = bass.ds(b * SEQ, SEQ)
                pool.tensor_copy(k.x_high[:, cols], x3T[p][:]).then_inc(s["x_high"], 1)
                pool.wait_ge(s["x_high"], made(b))
                k.settle(pool)
                pool.tensor_tensor(k.x_low[:, cols], x3T[p][:], k.x_high[:, cols].bitcast(F32), ALU.subtract
                                   ).then_inc(s["x_low"], 1)

            pipeline(pool, [(5, residual), (0, norm), (6, split), (1, square), (1, lows), (5, gate), (3, place_values),
                            (5, norm1), (5, keep)])
            pool.wait_ge(s["kept"], made(SEQS - 1))
            pool.wait_ge(s["x_low"], made(SEQS - 1))

        @block.scalar
        def _(act):
            for name in "dist logd w".split():
                credit(act, s[name], per.get(name, 1))
            act.wait_ge(s_set, 5)

            def weights(b, p):
                for n in range(PARTS):
                    part = w[p][:, n * PART:(n + 1) * PART, :]
                    act.wait_ge(s["d"], made(b, (n + 1) * PART, HEADS))
                    nc.scalar.activation(part, part, ACT.Sqrt).then_inc(s["dist"], 1)
                act.preload_act_table_set("natural_log_exp_and_others")
                for n in range(PARTS):
                    part = w[p][:, n * PART:(n + 1) * PART, :]
                    act.wait_ge(s["dist"], made(b, n + 1, PARTS))
                    nc.scalar.activation(part, part, ACT.Ln, bias=eps[:, 0:1]).then_inc(s["logd"], 1)
                for n in range(PARTS):
                    part = w[p][:, n * PART:(n + 1) * PART, :]
                    act.wait_ge(s["logd"], made(b, n + 1, PARTS))
                    nc.scalar.activation(part, part, ACT.Exp, scale=-2.0).then_inc(s["w"], 1)

            pipeline(act, [(3, weights), (6, idle)])

        @block.vector
        def _(dve):
            for name in ("stats moments xn xnT qkvg high norms norms_high slots slotsT d avT rden0 rden o0 oT r stats1 "
                         "moments1 x3 x3T logits").split():
                credit(dve, s[name], per.get(name, 1))
            dve.wait_ge(s_set, 5)

            def norm_a(b, p):
                statistics(k, dve, lambda j: k.x[:, tile_of(b, j), :], stats[p]).then_inc(s["stats"], 1)

            def norm_b(b, p):
                dve.wait_ge(s["stats"], made(b))
                moments(k, dve, stats[p], mv[p]).then_inc(s["moments"], 1)

            def norm_x(b, p):
                dve.wait_ge(s["rstd"], made(b))
                after(dve, s["xnT_p"], freed(b))
                for j in range(TPS):
                    last = normalise(nc, xn[p][:, j:j + 1, :], k.x[:, tile_of(b, j), :], mv[p], rstd[p], j)
                last.then_inc(s["xn"], 1)

            def norm_t(b, p):
                dve.wait_ge(s["xnT_p"], made(b))
                after(dve, s["p_p"], freed(b, TPS, TPS))
                nc.vector.tensor_copy(xnT[p][:], t_bank[:, 0:SEQ]).then_inc(s["xnT"], 1)

            def build(j):
                def stage(b, p):
                    dve.wait_ge(s["p_p"], made(b, j + 1, TPS))
                    after(dve, s["lows"], freed(b))
                    after(dve, s["squares"], freed(b))
                    nc.vector.tensor_tensor(qk[p][:, j].rearrange("p q h w -> p (q h w)"), p_bank[:, 0:2 * D],
                                            k.row["b_in"][:, 0:2 * D], ALU.add)
                    nc.vector.tensor_tensor(values_all[:, tile_of(b, j), :, :].rearrange("p t h w -> p t (h w)"),
                                            p_bank[:, 2 * D:3 * D].unsqueeze(1),
                                            k.row["b_in"][:, 2 * D:3 * D].unsqueeze(1), ALU.add)
                    nc.vector.tensor_tensor(gates[:, tile_of(b, j), :], p_bank[:, 3 * D:4 * D].unsqueeze(1),
                                            k.row["b_in"][:, 3 * D:4 * D].unsqueeze(1), ALU.add).then_inc(s["qkvg"], 1)
                return stage

            def high(b, p):
                after(dve, s["slots_p"], freed(b, FILLS, FILLS))
                dve.wait_ge(s["qkvg"], made(b, TPS, TPS))
                nc.vector.tensor_copy(slots[p][:].rearrange("p j q h w -> p (j q h) w")[:, :, 0:DH].bitcast(F32R),
                                      qk[p][:].rearrange("p j q h w -> p (j q h) w"))
                for q, at in ((QUERY, DH), (KEY, 2 * DH)):
                    last = nc.vector.tensor_copy(slots[p][:, :, q, :, at:at + DH].bitcast(F32R), qk[p][:, :, q])
                last.then_inc(s["high"], 1)

            def norms_a(b, p):
                dve.wait_ge(s["squares"], made(b))
                nc.vector.tensor_reduce(norms[p][:].rearrange("p j q h -> p (j q h)"),
                                        squares[p][:].rearrange("p j q h w -> p (j q h) w"), AX, ALU.add).then_inc(s["norms"], 1)

            def norms_b(b, p):
                dve.wait_ge(s["norms"], made(b))
                for q, at in ((QUERY, Q_NORM), (KEY, K_NORM)):
                    last = nc.vector.tensor_copy(slots[p][:, :, q, :, at].bitcast(F32R), norms[p][:, :, q])
                last.then_inc(s["norms_high"], 1)

            def norms_c(b, p):
                dve.wait_ge(s["norms_high"], made(b))
                for q, at in ((QUERY, Q_NORM), (KEY, K_NORM)):
                    last = nc.vector.tensor_tensor(slots[p][:, :, q, :, at + 1], norms[p][:, :, q], slots[p][:, :, q, :, at],
                                                   ALU.subtract)
                last.then_inc(s["slots"], 1)

            def slots_t(f):
                def stage(b, p):
                    dve.wait_ge(s["slots_p"], made(b, f + 1, FILLS))
                    after(dve, s["d_p"], freed(b, HEADS, HEADS))
                    nc.vector.tensor_copy(slotsT[p][:, 2 * f:2 * f + 2].rearrange("p g j t -> p (g j t)"), t_bank[:]
                                          ).then_inc(s["slotsT"], 1)
                return stage

            def distances(h):
                def stage(b, p):
                    dve.wait_ge(s["d_p"], made(b, h + 1, HEADS))
                    nc.vector.tensor_scalar(w[p][:, h, :], d_banks[h % D_BANKS][:], -2.0, 0.0, ALU.mult, ALU.max
                                            ).then_inc(s["d"], 1)
                return stage

            def applied(half):
                def stage(b, p):
                    dve.wait_ge(s["avT_p"], made(b, half + 1, 2))
                    after(dve, s["av_p"], freed(b))
                    nc.vector.tensor_copy(avT[p][:, 2 * half:2 * half + 2].rearrange("p g t -> p (g t)"),
                                          avT_banks[half][:]).then_inc(s["avT"], 1)
                return stage

            av = [bank[:].rearrange("p (h w) -> p h w", w=HW) for bank in av_banks]

            def divide_a(b, p):
                dve.wait_ge(s["av_p"], made(b))
                for t in range(TPS):
                    last = nc.vector.tensor_scalar(rden[p][:, t], av[t][:, :, DH], SHEP_EPS, None, ALU.add)
                last.then_inc(s["rden0"], 1)

            def divide_b(b, p):
                dve.wait_ge(s["rden0"], made(b))
                nc.vector.reciprocal(rden[p][:], rden[p][:]).then_inc(s["rden"], 1)

            def divide_c(b, p):
                dve.wait_ge(s["rden"], made(b))
                after(dve, s["oT_p"], freed(b))
                for t in range(TPS):
                    last = nc.vector.tensor_tensor(o[p][:, t].rearrange("p (h w) -> p h w", w=DH), av[t][:, :, 0:DH],
                                                   spread(rden[p][:, t], DH), ALU.mult)
                last.then_inc(s["o0"], 1)

            def out_t(b, p):
                dve.wait_ge(s["oT_p"], made(b))
                after(dve, s["out_p"], freed(b))
                nc.vector.tensor_copy(oT[p][:], out_bank[:, 0:SEQ]).then_inc(s["oT"], 1)

            def add(b, p):
                dve.wait_ge(s["out_p"], made(b))
                dve.wait_ge(s["xb"], made(b))
                nc.vector.tensor_tensor(r[p][:], out_bank[:, SEQ:2 * SEQ].rearrange("p (j d) -> p j d", j=TPS), xb[p][:],
                                        ALU.add).then_inc(s["r"], 1)

            def norm1_a(b, p):
                dve.wait_ge(s["r"], made(b))
                statistics(k, dve, lambda j: r[p][:, j, :], stats1[p]).then_inc(s["stats1"], 1)

            def norm1_b(b, p):
                dve.wait_ge(s["stats1"], made(b))
                moments(k, dve, stats1[p], mv1[p]).then_inc(s["moments1"], 1)

            def norm1_x(b, p):
                dve.wait_ge(s["rstd1"], made(b))
                after(dve, s["x3T_p"], freed(b))
                after(dve, s["kept"], freed(b))
                for j in range(TPS):
                    last = normalise(nc, x3[p][:, j:j + 1, :], r[p][:, j:j + 1, :], mv1[p], rstd1[p], j)
                last.then_inc(s["x3"], 1)

            def norm1_t(b, p):
                dve.wait_ge(s["x3T_p"], made(b))
                after(dve, s["logits_p"], freed(b))
                after(dve, s["x_low"], freed(b))
                nc.vector.tensor_copy(x3T[p][:], out_bank[:, 0:SEQ]).then_inc(s["x3T"], 1)

            def logits(b, p):
                dve.wait_ge(s["logits_p"], made(b))
                nc.vector.tensor_copy(k.logits[:, bass.ds(b * TPS, TPS), :],
                                      out_bank[:, SEQ:SEQ + TPS * E].rearrange("p (j e) -> p j e", j=TPS)
                                      ).then_inc(s["logits"], 1)

            pipeline(dve, among_heads(lambda h: (2, distances(h)), {0: [(5, applied(1)), (6, norm1_t)], 1: [(1, build(0))], 2: [(0, norm_a), (6, logits)], 3: [(5, divide_a), (0, norm_b)],
4: [(1, build(1)), (5, divide_b)], 5: [(5, divide_c), (1, high)], 6: [(0, norm_x)], 7: [(4, applied(0))], 8: [(1, norms_a)],
9: [(1, norms_b), (5, out_t)], 10: [(1, norms_c), (0, norm_t)], 11: [(1, slots_t(0)), (5, add)], 12: [(1, slots_t(1)), (5, norm1_a)],
13: [(1, slots_t(2)), (5, norm1_b)], 14: [(1, slots_t(3)), (5, norm1_x)] }))

        @block.tensor
        def _(pe):
            for name in "xnT_p p_p slots_p d_p avT_p av_p oT_p out_p x3T_p logits_p".split():
                credit(pe, s[name], per.get(name, 1))

            def norm_t(b, p):
                pe.wait_ge(s["xn"], made(b))
                pe.wait_ge(s["xnT"], made(b - 1))
                if not isinstance(b, int) or b >= 5:
                    pe.wait_ge(s["o0"], made(b - 5))
                after(pe, s["slotsT"], made(b - 1, 0, FILLS))
                for j in range(TPS):
                    last = nc.tensor.transpose(t_bank[:, j * P:(j + 1) * P], xn[p][:, j, :], k.ident)
                last.then_inc(s["xnT_p"], 1)

            def project(j):
                def stage(b, p):
                    pe.wait_ge(s["xnT"], made(b))
                    after(pe, s["qkvg"], made(b, j, TPS))
                    nc.tensor.matmul(p_bank[:], xnT[p][:, j * P:(j + 1) * P], k.w_in[:], start=True, stop=True
                                     ).then_inc(s["p_p"], 1)
                return stage

            def slots_t(f):
                def stage(b, p):
                    pe.wait_ge(s["slots"], made(b))
                    pe.wait_ge(s["lows"], made(b))
                    after(pe, s["slotsT"], made(b, f, FILLS))
                    pe.wait_ge(s["xnT"], made(b + 1) if not isinstance(b, int) or b + 1 < SEQS else made(b))
                    for g in range(2):
                        q, first = divmod((2 * f + g) * HG, HEADS)
                        for j in range(TPS):
                            last = nc.tensor.transpose(
                                t_bank[:, (g * TPS + j) * P:(g * TPS + j + 1) * P],
                                slots[p][:, j, q, first:first + HG, :].rearrange("p h w -> p (h w)"), k.ident)
                    last.then_inc(s["slots_p"], 1)
                return stage

            def distances(h):
                def stage(b, p):
                    if h == 0:
                        pe.wait_ge(s["slotsT"], made(b, FILLS, FILLS))
                    g, at = h // HG, h % HG * HW
                    before = [i for i in range(h - HEADS, h) if i % HEADS % D_BANKS == h % D_BANKS][-1]
                    after(pe, s["d"], made(b, before + 1, HEADS))
                    for kt in range(TPS):
                        last = nc.tensor.matmul(d_banks[h % D_BANKS][:, kt * SEQ:(kt + 1) * SEQ],
                                                slotsT[p][at:at + USED, GROUPS + g, kt, :],
                                                slotsT[p][at:at + USED, g, :, :].rearrange("p j t -> p (j t)"),
                                                start=True, stop=True)
                    last.then_inc(s["d_p"], 1)
                return stage

            def apply(h):
                half, g, at = h // (HEADS // 2), h // HG, h % HG * HW

                def stage(b, p):
                    if h % PART == 0:
                        pe.wait_ge(s["w"], made(b, h // PART + 1, PARTS))
                    if h == 0:
                        pe.wait_ge(s["values"], made(b))
                    if h % (HEADS // 2) == 0:
                        after(pe, s["avT"], made(b - 1, half + 1, 2))
                    if h == HEADS // 2:
                        pe.wait_ge(s["o0"], made(b - 1))
                    for kt in range(TPS):
                        last = nc.tensor.matmul(avT_banks[half][at:at + HW, g % 2 * SEQ:(g % 2 + 1) * SEQ],
                                                values[p][:, kt, h, :], w[p][:, h, kt * SEQ:(kt + 1) * SEQ],
                                                start=(kt == 0), stop=(kt == TPS - 1), tile_position=(0, at))
                    if h % (HEADS // 2) == HEADS // 2 - 1:
                        last.then_inc(s["avT_p"], 1)
                return stage

            def av_t(b, p):
                pe.wait_ge(s["avT"], made(b, 2, 2))
                behind = b + 3 if not isinstance(b, int) else min(b + 3, SEQS - 1)
                pe.wait_ge(s["slotsT"], made(behind, FILLS, FILLS))
                for t in range(TPS):
                    for g in range(GROUPS):
                        last = nc.tensor.transpose(av_banks[t][:, g * P:(g + 1) * P], avT[p][:, g, t * P:(t + 1) * P], k.ident)
                last.then_inc(s["av_p"], 1)

            def out_t(b, p):
                pe.wait_ge(s["o"], made(b))
                pe.wait_ge(s["logits"], made(b - 1))
                for j in range(TPS):
                    last = nc.tensor.transpose(out_bank[:, j * P:(j + 1) * P], o[p][:, j, :], k.ident)
                last.then_inc(s["oT_p"], 1)

            def out(b, p):
                pe.wait_ge(s["oT"], made(b))
                for j in range(TPS):
                    last = nc.tensor.matmul(out_bank[:, SEQ + j * D:SEQ + (j + 1) * D], oT[p][:, j * P:(j + 1) * P],
                                            k.w_out[:], start=True, stop=True)
                last.then_inc(s["out_p"], 1)

            def norm1_t(b, p):
                pe.wait_ge(s["x3"], made(b))
                for j in range(TPS):
                    last = nc.tensor.transpose(out_bank[:, j * P:(j + 1) * P], x3[p][:, j, :], k.ident)
                last.then_inc(s["x3T_p"], 1)

            def logits(b, p):
                pe.wait_ge(s["x3T"], made(b))
                pe.wait_ge(s["r"], made(b))
                for j in range(TPS):
                    at = SEQ + j * E
                    last = nc.tensor.matmul(out_bank[:, at:at + E], x3T[p][:, j * P:(j + 1) * P], k.w_router[:, 1, :],
                                            start=True, stop=True)
                last.then_inc(s["logits_p"], 1)

            pipeline(pe, among_heads(lambda h: [(4, apply(h)), (2, distances(h))], {0: [(1, project(0)), (6, norm1_t)], 1: [(5, av_t)], 2: [(6, logits)], 4: [(1, project(1))], 8: [(5, out_t), (0, norm_t)], 10: [(5, out)],
11: [(1, slots_t(0))], 12: [(1, slots_t(1))], 13: [(1, slots_t(2))], 14: [(1, slots_t(3))]}))


def layer1_moe(k):
    nc = k.nc
    BLOCK = 512
    BLOCKS, NCH = TOKENS // BLOCK, len(CHUNKS)
    UNITS = BLOCKS * NCH
    W13, W2 = 2 * HID, NCH * D
    RING = 3
    CAST, LOW, DOWN = 1, 1, 2
    CUT = NCH
    with ExitStack() as c:
        sb = lambda name, shape, dt=F32: c.enter_context(nc.sbuf_tensor("m_" + name, shape, dt))
        pair = lambda name, shape, dt=F32: [sb(f"{name}{i}", shape, dt) for i in range(2)]
        ring = lambda name, shape, dt=F32: [sb(f"{name}{i}", shape, dt) for i in range(RING)]
        raw, high, low = pair("raw", [P, W13 + W2]), pair("high", [P, W13 + W2], F32R), pair("low", [P, W13 + W2], F32R)
        share = pair("share", [P, TOKENS])
        silu, h = ring("silu", [P, BLOCK]), ring("h", [P, BLOCK])
        h_high, h_low = ring("h_high", [P, BLOCK], F32R), ring("h_low", [P, BLOCK], F32R)
        wy = pair("wy", [P, BLOCK])
        yT = k.yT
        cwT = sb("cwT", [P, P])
        shares = nc.dram_tensor("shares", [E, TILES, P], F32).ap()
        gate_banks, up_banks, y_banks = k.psum[0:2], k.psum[2:4], k.psum[4:6]
        names = "raw0 raw1 share0 share1 high low gate_p up_p silu h h_high h_low h_read wy yT".split()
        s = {n: k.sem("m_" + n) for n in names}
        per = {n: UNITS for n in "gate_p up_p silu h h_high h_low h_read".split()} | dict(wy=BLOCKS, yT=BLOCKS)
        s_cwT_p, s_cwT, s_shares, s_zero = k.sem("m_cwT_p"), k.sem("m_cwT"), k.sem("m_shares"), k.sem("m_zero")
        route_on_scalar, route_on_vector, s_routed = router(k, c, 1)
        block = c.enter_context(nc.Block(no_gpsimd_drain=True))

        def products(work):
            most = max(lag for lag, _ in work)

            def stage(b, p, units):
                for u in units:
                    for lag, step in work:
                        if u >= lag:
                            step(b, p, u - lag)
                        elif not isinstance(b, int) or b > 0:
                            step(b - 1, 1 - p, UNITS + u - lag)

            def rest():
                for u in range(most):
                    for lag, step in work:
                        if u < lag:
                            step(E - 1, (E - 1) % 2, UNITS + u - lag)
            return (lambda b, p: stage(b, p, range(CUT))), (lambda b, p: stage(b, p, range(CUT, UNITS))), rest

        @block.sync
        def _(sp):
            for name in "raw0 raw1 share0 share1".split():
                sp.sem_inc(s[name], 1)

            def fetch(b, p):
                after(sp, s["low"], freed(b))
                sp.dma_start(raw[p][:, 0:W13], k.dram["w13"][:, bass.ds(b * W13, W13)]).then_inc(s[f"raw{p}"], 16)
                for ch, (at, n) in enumerate(CHUNKS):
                    sp.dma_start(raw[p][0:n, W13 + ch * D:W13 + (ch + 1) * D],
                                 k.dram["w2"][at:at + n, bass.ds(b * D, D)]).then_inc(s[f"raw{p}"], 16)
                if isinstance(b, int) and b == 0:
                    sp.wait_ge(s_cwT, 1)
                    sp.dma_start(shares.rearrange("e t p -> (e t) p"), cwT[:]).then_inc(s_shares, 16)
                    sp.wait_ge(s_shares, 16)
                after(sp, s["wy"], freed(b, BLOCKS, BLOCKS))
                row = shares[bass.ds(b, 1)].rearrange("e t p -> e (t p)")
                sp.dma_start(share[p][:], row.to_broadcast([P, TOKENS])).then_inc(s[f"share{p}"], 16)

            pipeline(sp, [(0, fetch), (2, idle)], E, 2)

        @block.gpsimd
        def _(pool):
            for name in ("low", "yT"):
                credit(pool, s[name], per.get(name, 1))
            pool.memset(yT[:], 0.0).then_inc(s_zero, 1)
            pool.wait_ge(s_zero, 1)

            def split(b, p):
                pool.wait_ge(s["high"], made(b))
                after(pool, s["h_read"], freed(b, UNITS, UNITS))
                pool.tensor_tensor(low[p][:, 0:W13 + 2 * D], raw[p][:, 0:W13 + 2 * D], high[p][:, 0:W13 + 2 * D].bitcast(F32),
                                   ALU.subtract)
                n = CHUNKS[-1][1]
                pool.tensor_tensor(low[p][0:n, W13 + 2 * D:], raw[p][0:n, W13 + 2 * D:], high[p][0:n, W13 + 2 * D:].bitcast(F32),
                                   ALU.subtract).then_inc(s["low"], 1)

            def add(b, blocks):
                for t in blocks:
                    pool.wait_ge(s["wy"], made(b, t + 1, BLOCKS))
                    after(pool, s["yT"], made(b - 1, t + 1, BLOCKS))
                    cols = slice(t * BLOCK, (t + 1) * BLOCK)
                    pool.tensor_tensor(yT[:, cols], yT[:, cols], wy[t % 2][:], ALU.add).then_inc(s["yT"], 1)

            pipeline(pool, [(2, lambda b, p: add(b, range(1))), (1, split), (2, lambda b, p: add(b, range(1, BLOCKS)))], E, 2)
            pool.wait_ge(s["yT"], made(E - 1, BLOCKS, BLOCKS))

        @block.scalar
        def _(act):
            for name in ("high", "silu", "h_high"):
                credit(act, s[name], per.get(name, 1))
            route_on_scalar(act)

            def split(b, p):
                act.wait_ge(s[f"raw{p}"], landed(b, p, 1 + NCH))
                after(act, s["h_read"], freed(b, UNITS, UNITS))
                nc.scalar.activation(high[p][:, 0:W13 + 2 * D], raw[p][:, 0:W13 + 2 * D], ACT.Copy)
                n = CHUNKS[-1][1]
                nc.scalar.activation(high[p][0:n, W13 + 2 * D:], raw[p][0:n, W13 + 2 * D:], ACT.Copy).then_inc(s["high"], 1)

            def gate(b, p, u):
                n = CHUNKS[u % NCH][1]
                act.wait_ge(s["gate_p"], made(b, u + 1, UNITS))
                after(act, s["h"], made(b, u + 1 - RING, UNITS))
                nc.scalar.activation(silu[u % RING][0:n, :], gate_banks[u % 2][0:n, :], ACT.Silu).then_inc(s["silu"], 1)

            def cast(b, p, u):
                n = CHUNKS[u % NCH][1]
                act.wait_ge(s["h"], made(b, u + 1, UNITS))
                after(act, s["h_read"], made(b, u + 1 - RING, UNITS))
                nc.scalar.activation(h_high[u % RING][0:n, :], h[u % RING][0:n, :], ACT.Copy).then_inc(s["h_high"], 1)

            begin, go_on, rest = products([(0, gate), (CAST, cast)])
            pipeline(act, [(2, begin), (1, split), (2, go_on)], E, 2)
            rest()

        @block.vector
        def _(dve):
            for name in ("h", "h_low", "wy"):
                credit(dve, s[name], per.get(name, 1))
            route_on_vector(dve)
            dve.wait_ge(s_cwT_p, 1)
            nc.vector.tensor_copy(cwT[:], k.psum[6][:, 0:P]).then_inc(s_cwT, 1)

            def multiply(b, p, u):
                n = CHUNKS[u % NCH][1]
                dve.wait_ge(s["silu"], made(b, u + 1, UNITS))
                dve.wait_ge(s["up_p"], made(b, u + 1, UNITS))
                after(dve, s["h_high"], made(b, u + 1 - RING, UNITS))
                nc.vector.tensor_tensor(h[u % RING][0:n, :], up_banks[u % 2][0:n, :], silu[u % RING][0:n, :], ALU.mult
                                        ).then_inc(s["h"], 1)

            def split(b, p, u):
                n = CHUNKS[u % NCH][1]
                dve.wait_ge(s["h_high"], made(b, u + 1, UNITS))
                after(dve, s["h_read"], made(b, u + 1 - RING, UNITS))
                nc.vector.tensor_tensor(h_low[u % RING][0:n, :], h[u % RING][0:n, :], h_high[u % RING][0:n, :].bitcast(F32),
                                        ALU.subtract).then_inc(s["h_low"], 1)

            def weigh(b, p, u):
                if u % NCH < NCH - 1:
                    return
                t = u // NCH
                dve.wait_ge(s["h_read"], made(b, u + 1, UNITS))
                dve.wait_ge(s[f"share{p}"], landed(b, p))
                after(dve, s["yT"], made(b, t - 1, BLOCKS))
                nc.vector.tensor_tensor(wy[t % 2][:], y_banks[t % 2][:], share[p][:, t * BLOCK:(t + 1) * BLOCK], ALU.mult
                                        ).then_inc(s["wy"], 1)

            begin, go_on, rest = products([(0, multiply), (LOW, split), (DOWN + 1, weigh)])
            pipeline(dve, [(2, begin), (2, go_on)], E, 2)
            rest()

        @block.tensor
        def _(pe):
            for name in ("gate_p", "up_p", "h_read"):
                credit(pe, s[name], per.get(name, 1))
            pe.wait_ge(s_routed, 1)
            nc.tensor.transpose(k.psum[6][:, 0:P], k.cw_by_expert[:].rearrange("p e t -> p (e t)"), k.ident).then_inc(s_cwT_p, 1)

            def product(out, at, n, cols, rows, parts, start, stop):
                for i, (w, x) in enumerate(parts):
                    last = nc.tensor.matmul(out, w[0:rows, at:at + n], x[0:rows, cols], start=start and i == 0,
                                            stop=stop and i == len(parts) - 1)
                return last

            def up(b, p, u):
                ch, t = u % NCH, u // NCH
                at, n = CHUNKS[ch]
                cols = slice(t * BLOCK, (t + 1) * BLOCK)
                parts = [(high[p], k.x_high), (high[p], k.x_low), (low[p], k.x_high)]
                pe.wait_ge(s["low"], made(b))
                after(pe, s["silu"], made(b, u - 1, UNITS))
                product(gate_banks[u % 2][0:n, :], at, n, cols, P, parts, True, True).then_inc(s["gate_p"], 1)
                after(pe, s["h"], made(b, u - 1, UNITS))
                product(up_banks[u % 2][0:n, :], HID + at, n, cols, P, parts, True, True).then_inc(s["up_p"], 1)

            def down(b, p, u):
                ch, t = u % NCH, u // NCH
                n = CHUNKS[ch][1]
                pe.wait_ge(s["h_low"], made(b, u + 1, UNITS))
                if ch == 0:
                    after(pe, s["wy"], made(b, t - 1, BLOCKS))
                parts = [(high[p], h_high[u % RING]), (high[p], h_low[u % RING]), (low[p], h_high[u % RING])]
                last = product(y_banks[t % 2][:], W13 + ch * D, D, slice(0, BLOCK), n, parts, ch == 0, ch == NCH - 1)
                last.then_inc(s["h_read"], 1)

            begin, go_on, rest = products([(0, up), (DOWN, down)])
            pipeline(pe, [(2, begin), (2, go_on)], E, 2)
            rest()



def last_norm_moe(k):
    nc, yT = k.nc, k.yT
    with ExitStack() as c:
        sb = lambda name, shape: c.enter_context(nc.sbuf_tensor("f_" + name, shape, F32))
        pair = lambda name, shape: [sb(f"{name}{i}", shape) for i in range(2)]
        y, r, out = pair("y", [P, SEQ]), pair("r", [P, TPS, D]), pair("out", [P, TPS, D])
        stats, mv, rstd = pair("stats", [P, TPS, 6]), pair("mv", [P, TPS, 2]), pair("rstd", [P, TPS])
        banks = k.psum[0:2]
        s = {n: k.sem("f_" + n) for n in "y y_p r stats moments var rstd out".split()}
        per = {}
        s_out = [k.sem(f"f_stored{p}") for p in range(2)]
        block = c.enter_context(nc.Block(no_gpsimd_drain=True))
        out_dram = k.out.rearrange("b (j p) d -> p (b j) d", p=P)

        @block.scalar
        def _(act):
            credit(act, s["y"])

            def fetch(b, p):
                after(act, s["y_p"], freed(b))
                k.settle(act)
                nc.scalar.activation(y[p][:], yT[:, bass.ds(b * SEQ, SEQ)], ACT.Copy).then_inc(s["y"], 1)

            pipeline(act, [(0, fetch), (3, idle)], head=1)

        @block.vector
        def _(dve):
            for name in "r stats moments out".split():
                credit(dve, s[name])

            def add(b, p):
                dve.wait_ge(s["y_p"], made(b))
                after(dve, s["out"], freed(b))
                nc.vector.tensor_tensor(r[p][:], banks[p][:, 0:SEQ].rearrange("p (j d) -> p j d", j=TPS),
                                        k.x[:, bass.ds(b * TPS, TPS), :], ALU.add).then_inc(s["r"], 1)

            def norm_a(b, p):
                dve.wait_ge(s["r"], made(b))
                statistics(k, dve, lambda j: r[p][:, j, :], stats[p]).then_inc(s["stats"], 1)

            def norm_b(b, p):
                dve.wait_ge(s["stats"], made(b))
                moments(k, dve, stats[p], mv[p]).then_inc(s["moments"], 1)

            def norm_x(b, p):
                dve.wait_ge(s["rstd"], made(b))
                if not isinstance(b, int) or b >= 2:
                    dve.wait_ge(s_out[p], (b - p) * 8 + 1)
                for j in range(TPS):
                    last = normalise(nc, out[p][:, j:j + 1, :], r[p][:, j:j + 1, :], mv[p], rstd[p], j)
                last.then_inc(s["out"], 1)

            pipeline(dve, [(2, norm_b), (3, norm_x), (1, add), (1, norm_a)], head=1)

        @block.gpsimd
        def _(pool):
            for name in ("var", "rstd"):
                credit(pool, s[name])

            def norm(b, p):
                pool.wait_ge(s["moments"], made(b))
                rstd_of(k, pool, b, rstd[p], mv[p], s["var"]).then_inc(s["rstd"], 1)

            pipeline(pool, [(2, norm), (3, idle)], head=1)

        @block.tensor
        def _(pe):
            credit(pe, s["y_p"])

            def turn(b, p):
                pe.wait_ge(s["y"], made(b))
                after(pe, s["r"], freed(b))
                for j in range(TPS):
                    last = nc.tensor.transpose(banks[p][:, j * P:(j + 1) * P], y[p][:, j * P:(j + 1) * P], k.ident)
                last.then_inc(s["y_p"], 1)

            pipeline(pe, [(0, turn), (3, idle)], head=1)

        @block.sync
        def _(sp):
            for sem in s_out:
                sp.sem_inc(sem, 1)

            def store(b, p):
                sp.wait_ge(s["out"], made(b))
                sp.dma_start(out_dram[:, bass.ds(b * TPS, TPS), :], out[p][:]).then_inc(s_out[p], 16)

            pipeline(sp, [(3, store)], head=1)
            for p in range(2):
                sp.wait_ge(s_out[p], landed(SEQS - 2 + p, p))


def build(nc, dram, out):
    with ExitStack() as ctx:
        k = Kernel(nc, ctx, dram, out)
        layer0_attention(k)
        layer0_experts(k)
        layer1_attention(k)
        layer1_moe(k)
        last_norm_moe(k)




def layouts(i):
    import numpy as np

    f = lambda n: np.asarray(i[n])
    b_qkv = f("L0_attn_b_qkv").reshape(3, D)
    cols = np.stack([b_qkv[0], b_qkv[1], f("L0_attn_b_gate"), f("L0_attn_ln_g"), f("L0_attn_ln_b")] + [np.zeros(D, np.float32)] * 3, 1)
    order = np.arange(4 * D).reshape(HEADS, 4, DH).transpose(1, 0, 2).reshape(-1)
    rows = [np.concatenate([b_qkv[2]] * TPS), f("L0_attn_b_proj"), np.concatenate([f("L0_ffn_router_b")] * TILES),
            f("L1_attn_b_in")[order], f("L1_attn_b_out")]
    t = np.arange(P)
    causal = (t[:, None] <= t[None, :]).astype(np.float32)
    rank = np.broadcast_to(np.tile(np.arange(E, 0, -1, dtype=np.float32), TILES), (P, TILES * E))
    return {
        "x": f("L0_attn_x"),
        "consts": np.concatenate([np.eye(P, dtype=np.float32), causal, np.ones((P, P), np.float32), causal, rank], 1),
        "cols": cols,
        "rows": np.broadcast_to(np.concatenate(rows), (P, sum(n for _, n in ROWS))),
        "w_qkvg": np.concatenate([f("L0_attn_w_qkv"), f("L0_attn_w_gate")], 1),
        "w_proj": f("L0_attn_w_proj"),
        "w_router": np.stack([f("L0_ffn_router_w").T, f("L1_ffn_Wg").T], 1),
        "w_exp0": f("L0_ffn_expert_weights").transpose(1, 0, 2).reshape(D, E * D),
        "w_in": f("L1_attn_W_in").T[:, order],
        "w_out": f("L1_attn_W_out").T,
        "w13": np.concatenate([f("L1_ffn_W1"), f("L1_ffn_W3")], 1).transpose(2, 0, 1).reshape(D, E * 2 * HID),
        "w2": f("L1_ffn_W2").transpose(2, 0, 1).reshape(HID, E * D),
    }


def kernel(**inputs):
    import numpy as np
    import concourse.bacc as bacc
    from concourse.bass_utils import run_bass_kernel_spmd

    arrays = {name: np.ascontiguousarray(a) for name, a in layouts(inputs).items()}
    nc = bacc.Bacc("TRN2", target_bir_lowering=False, num_devices=1)
    dram = {name: nc.dram_tensor(name, a.shape, F32, kind="ExternalInput").ap() for name, a in arrays.items()}
    out = nc.dram_tensor("out", (SEQS, SEQ, D), F32, kind="ExternalOutput").ap()
    build(nc, dram, out)
    r = run_bass_kernel_spmd(nc, [arrays], core_ids=[0])
    return r.results[0]["out"]
```

```python
from contextlib import ExitStack

import concourse.bass as bass
from concourse import mybir

F32 = mybir.dt.float32
F32R = mybir.dt.float32r
ALU = mybir.AluOpType
ACT = mybir.ActivationFunctionType
AX = mybir.AxisListType.X

P = 128
SEQS, SEQ, D = 8, 256, 128
TOKENS = SEQS * SEQ
TILES = TOKENS // P
TPS = SEQ // P
E = 8
HEADS, DH = 16, 8
HW = 32
HG = P // HW
GROUPS = HEADS // HG
HID = 352
CHUNKS = [(0, 128), (128, 128), (256, 96)]
MOE_COLS = 2 * HID + len(CHUNKS) * D
LN_EPS = 1e-5
DEN_EPS = 1e-6
TOPK_EPS = 1e-10
SHEP_EPS = 1e-4
MOE_EPS = 1e-20


def made(b, i=1, per=1):
    return (b + 2) * per + i


def freed(b, i=1, per=1):
    return b * per + i


def credit(eng, sem, per=1):
    eng.sem_inc(sem, 2 * per)


def landed(b, p, dmas=1):
    return (b - p) * (8 * dmas) + (16 * dmas + 1)


def after(eng, sem, value):
    if not isinstance(value, int) or value > 0:
        eng.wait_ge(sem, value)


def pipeline(eng, stages, n=SEQS, head=0):
    first = max(lag for lag, _ in stages) + head
    assert n > first and (n - first) % 2 == 0

    def irregular(i):
        for lag, stage in stages:
            if 0 <= i - lag < n:
                stage(i - lag, (i - lag) % 2)

    for i in range(first):
        irregular(i)
    with eng.Fori(0, (n - first) // 2) as pairs:
        for u in range(2):
            for lag, stage in stages:
                o = first + u - lag
                stage(pairs * 2 + o, o % 2)
    for i in range(n, n + first - head):
        irregular(i)


def idle(b, p):
    pass


def among_heads(of_head, others):
    listed = []
    for h in range(HEADS):
        stages = of_head(h)
        listed += (stages if isinstance(stages, list) else [stages]) + others.get(h, [])
    return listed


def tile_of(t, j):
    return bass.ds(t * TPS + j, 1)


def spread(ap, n):
    return ap.unsqueeze(len(ap.shape)).to_broadcast([*ap.shape, n])


class Kernel:

    def __init__(self, nc, ctx, dram, out):
        self.sem = lambda name: ctx.enter_context(nc.semaphore(name))
        self.settled = self.sem("settled")
        self.nc, self.dram, self.out = nc, dram, out
        sb = lambda name, shape, dt=F32: ctx.enter_context(nc.sbuf_tensor("sb_" + name, shape, dt))
        self.x = sb("x", [P, TILES, D])
        self.spare = sb("spare", [P, TILES, D])
        self.consts = sb("consts", [P, dram["consts"].shape[1]])
        self.ident = self.consts[:, 0:P]
        self.mask = self.consts[:, P:4 * P]
        self.index_rank = self.consts[:, 4 * P:5 * P]
        self.cols = sb("cols", [P, 8])
        self.rows = sb("rows", [P, dram["rows"].shape[1]])
        o = 0
        self.row = {}
        for name, n in ROWS:
            self.row[name] = self.rows[:, o:o + n]
            o += n
        self.moe_raw0 = sb("moe_raw0", [P, MOE_COLS])
        self.w_proj = sb("w_proj", [P, D])
        self.w_router = sb("w_router", [P, 2, E])
        self.w_in = sb("w_in", [P, 4 * D])
        self.w_out = sb("w_out", [P, D])
        self.logits = sb("logits", [P, TILES, E])
        self.cw = sb("cw", [P, TILES, E])
        self.cw_by_expert = sb("cw_by_expert", [P, E, TILES])
        self.x_high, self.x_low = sb("x_high", [P, TOKENS], F32R), sb("x_low", [P, TOKENS], F32R)
        self.yT = sb("yT", [P, TOKENS])
        self.minus_half = sb("minus_half", [P, TPS])
        self.layer0 = ctx.enter_context(ExitStack())
        self.w_qkvg, self.w_exp0 = (self.layer0.enter_context(nc.sbuf_tensor("sb_" + name, [P, n * D], F32))
                                    for name, n in (("w_qkvg", 4), ("w_exp0", E)))
        self.loads = {"consts": self.consts, "cols": self.cols, "rows": self.rows, "w_qkvg": self.w_qkvg,
                      "w_proj": self.w_proj, "w_router": self.w_router, "w_exp0": self.w_exp0, "w_in": self.w_in,
                      "w_out": self.w_out}
        self.sb = sb
        self.psum = [ctx.enter_context(nc.psum_tensor(f"bank{i}", [P, 512], F32)) for i in range(8)]

    def end_layer0(self):
        self.layer0.close()
        self.moe_high0 = self.sb("moe_high0", [P, MOE_COLS], F32R)

    def settle(self, eng):
        eng.sem_inc(self.settled, 1)


ROWS = [("b_v", TPS * D), ("b_proj", D), ("b_router", TILES * E), ("b_in", 4 * D), ("b_out", D)]


def layer0_attention(k):
    nc = k.nc
    with ExitStack() as c:
        sb = lambda name, shape: c.enter_context(nc.sbuf_tensor("a_" + name, shape, F32))
        pair = lambda name, shape: [sb(f"{name}{i}", shape) for i in range(2)]
        stats, mv, rstd = pair("stats", [P, TPS, 6]), pair("mv", [P, TPS, 2]), pair("rstd", [P, TPS])
        xn, xnT = pair("xn", [P, TPS, D]), pair("xnT", [P, SEQ])
        qk, low, features = (pair(name, [P, 2 * SEQ]) for name in ("qk", "low", "features"))
        v, th = pair("v", [P, TPS, D]), pair("th", [P, SEQ])
        attn, numT, rden = pair("attn", [P, 3 * P]), pair("numT", [P, SEQ]), pair("rden", [P, TPS])
        xb = pair("xb", [P, TPS, D])
        stats1, mv1, rstd1 = pair("stats1", [P, TPS, 6]), pair("mv1", [P, TPS, 2]), pair("rstd1", [P, TPS])
        x1T, x1 = pair("x1T", [P, SEQ]), pair("x1", [P, TPS, D])
        ones = sb("ones", [P, 1])
        t_bank, qk_bank, gate_bank, attn_bank, num_bank, x1_bank, v_bank, proj_bank = k.psum

        s_first, s_x, s_now, s_w = (k.sem("a_" + name) for name in ("x_first", "x_in", "w_now", "w_in"))
        s_set = k.sem("a_set")
        names = ("stats moments var rstd xn xnT_p xnT gate_p qk_p v_p th qk v kg low exp features attn_p attn num_p numT "
                 "rden0 rden proj_p xb r stats1 moments1 var1 rstd1 x1 kept x1T_p x1T logits_p logits").split()
        s = {n: k.sem("a_" + n) for n in names}
        block = c.enter_context(nc.Block())
        NOW = "cols w_qkvg consts rows".split()
        LATER = "w_proj w_router w_exp0 w_in w_out".split()

        @block.sync
        def _(sp):
            x_in = k.dram["x"].rearrange("b (j p) d -> p (b j) d", p=P)
            sp.dma_start(k.x[:, 0:TPS, :], x_in[:, 0:TPS, :]).then_inc(s_first, 16)
            sp.dma_start(k.consts[:], k.dram["consts"]).then_inc(s_now, 16)
            for b in range(1, SEQS):
                sp.dma_start(k.x[:, TPS * b:TPS * b + TPS, :], x_in[:, TPS * b:TPS * b + TPS, :]).then_inc(s_x, 16)

        @block.scalar
        def _(act):
            for name in NOW:
                if name != "consts":
                    act.dma_start(k.loads[name][:], k.dram[name]).then_inc(s_now, 16)
            for name in LATER:
                act.dma_start(k.loads[name][:], k.dram[name]).then_inc(s_w, 16)
            for name in ("xnT", "th", "exp", "numT", "x1T", "qk"):
                credit(act, s[name])
            act.wait_ge(s_now, 16 * len(NOW))
            act.wait_ge(s_set, 4)

            def norm_t(b, p):
                act.wait_ge(s["xnT_p"], made(b))
                after(act, s["v_p"], freed(b))
                nc.scalar.activation(xnT[p][:], t_bank[:, 0:SEQ], ACT.Identity, scale=k.cols[:, 3:4],
                                     bias=k.cols[:, 4:5]).then_inc(s["xnT"], 1)

            def gate(b, p):
                act.wait_ge(s["gate_p"], made(b))
                after(act, s["kg"], freed(b))
                nc.scalar.activation(th[p][:], gate_bank[:, 0:SEQ], ACT.Tanh, scale=0.5,
                                     bias=k.cols[:, 6:7]).then_inc(s["th"], 1)

            def project(b, p):
                act.wait_ge(s["qk_p"], made(b))
                after(act, s["features"], freed(b))
                nc.scalar.activation(qk[p][:, 0:SEQ], qk_bank[:, 0:SEQ], ACT.Identity, bias=k.cols[:, 0:1])
                nc.scalar.activation(qk[p][:, SEQ:2 * SEQ], qk_bank[:, SEQ:2 * SEQ], ACT.Identity, scale=0.5,
                                     bias=k.cols[:, 5:6]).then_inc(s["qk"], 1)

            def exponentials(b, p):
                act.wait_ge(s["low"], made(b))
                nc.scalar.activation(low[p][:], low[p][:], ACT.Exp).then_inc(s["exp"], 1)

            def numerators(b, p):
                act.wait_ge(s["num_p"], made(b))
                after(act, s["proj_p"], freed(b))
                nc.scalar.activation(numT[p][:], num_bank[:, 0:SEQ], ACT.Copy).then_inc(s["numT"], 1)

            def turned(b, p):
                act.wait_ge(s["x1T_p"], made(b))
                after(act, s["logits_p"], freed(b))
                nc.scalar.activation(x1T[p][:], x1_bank[:, 0:SEQ], ACT.Copy).then_inc(s["x1T"], 1)

            pipeline(act, [(3, exponentials), (2, gate), (2, project), (1, norm_t), (4, numerators), (6, turned)])

        @block.gpsimd
        def _(pool):
            for name in ("var", "rstd", "xb", "var1", "rstd1", "kept"):
                credit(pool, s[name])
            pool.memset(k.minus_half[:], -0.5).then_inc(s_set, 1)
            pool.memset(ones[:], 1.0).then_inc(s_set, 1)
            pool.memset(k.yT[:], 0.0).then_inc(s_set, 1)
            pool.wait_ge(s_set, 3)
            pool.wait_ge(s_now, 16 * len(NOW))

            def norm(b, p):
                pool.wait_ge(s["moments"], made(b))
                rstd_of(k, pool, b, rstd[p], mv[p], s["var"]).then_inc(s["rstd"], 1)

            def residual(b, p):
                pool.wait_ge(s["stats"], made(b))
                after(pool, s["r"], freed(b))
                for j in range(TPS):
                    last = pool.tensor_tensor(xb[p][:, j:j + 1, :], k.x[:, tile_of(b, j), :], k.row["b_proj"].unsqueeze(1), ALU.add)
                last.then_inc(s["xb"], 1)

            def norm1(b, p):
                pool.wait_ge(s["moments1"], made(b))
                rstd_of(k, pool, b, rstd1[p], mv1[p], s["var1"]).then_inc(s["rstd1"], 1)

            def keep(b, p):
                pool.wait_ge(s["x1"], made(b))
                k.settle(pool)
                pool.tensor_copy(k.x[:, bass.ds(b * TPS, TPS), :], x1[p][:]).then_inc(s["kept"], 1)

            pipeline(pool, [(4, residual), (6, keep), (0, norm), (5, norm1)])

        @block.vector
        def _(dve):
            for name in ("stats moments xn v kg low features attn rden0 rden r stats1 moments1 x1 logits").split():
                credit(dve, s[name])
            dve.wait_ge(s_now, 16 * len(NOW))
            nc.vector.tensor_scalar(k.cols[:, 5:7], k.cols[:, 1:3], 0.5, None, ALU.mult).then_inc(s_set, 1)
            dve.wait_ge(s_first, 16)

            def norm_a(b, p):
                if not isinstance(b, int) or b > 0:
                    dve.wait_ge(s_x, 16 * (SEQS - 1))
                statistics(k, dve, lambda j: k.x[:, tile_of(b, j), :], stats[p]).then_inc(s["stats"], 1)

            def norm_b(b, p):
                dve.wait_ge(s["stats"], made(b))
                moments(k, dve, stats[p], mv[p]).then_inc(s["moments"], 1)

            def norm_x(b, p):
                dve.wait_ge(s["rstd"], made(b))
                after(dve, s["xnT_p"], freed(b))
                for j in range(TPS):
                    last = normalise(nc, xn[p][:, j:j + 1, :], k.x[:, tile_of(b, j), :], mv[p], rstd[p], j)
                last.then_inc(s["xn"], 1)

            def values(b, p):
                dve.wait_ge(s["v_p"], made(b))
                after(dve, s["num_p"], freed(b))
                nc.vector.tensor_tensor(v[p][:], v_bank[:, 0:SEQ].rearrange("p (j d) -> p j d", j=TPS),
                                        k.row["b_v"].rearrange("p (j d) -> p j d", j=TPS), ALU.add).then_inc(s["v"], 1)

            def gate(b, p):
                dve.wait_ge(s["th"], made(b))
                dve.wait_ge(s["qk"], made(b))
                keys = qk[p][:, SEQ:2 * SEQ]
                nc.vector.scalar_tensor_tensor(keys, th[p][:], 1.0, keys, ALU.add, ALU.mult).then_inc(s["kg"], 1)

            def lows(b, p):
                dve.wait_ge(s["kg"], made(b))
                nc.vector.tensor_scalar(low[p][:], qk[p][:], 0.0, None, ALU.min).then_inc(s["low"], 1)

            def features_of(b, p):
                dve.wait_ge(s["exp"], made(b))
                after(dve, s["attn_p"], freed(b))
                nc.vector.scalar_tensor_tensor(features[p][:], qk[p][:], 1.0, low[p][:], ALU.add, ALU.max
                                               ).then_inc(s["features"], 1)

            def mask(b, p):
                dve.wait_ge(s["attn_p"], made(b))
                after(dve, s["num_p"], freed(b))
                nc.vector.tensor_tensor(attn[p][:], attn_bank[:, 0:3 * P], k.mask, ALU.mult).then_inc(s["attn"], 1)

            def denominators(b, p):
                dve.wait_ge(s["numT"], made(b))
                nc.vector.tensor_scalar(rden[p][:], num_bank[:, SEQ:SEQ + TPS], DEN_EPS, None, ALU.add).then_inc(s["rden0"], 1)

            def inverses(b, p):
                dve.wait_ge(s["rden0"], made(b))
                nc.vector.reciprocal(rden[p][:], rden[p][:]).then_inc(s["rden"], 1)

            def add(b, p):
                dve.wait_ge(s["proj_p"], made(b))
                dve.wait_ge(s["rden"], made(b))
                dve.wait_ge(s["xb"], made(b))
                for j in range(TPS):
                    last = nc.vector.scalar_tensor_tensor(k.spare[:, tile_of(b, j), :], proj_bank[:, j * D:(j + 1) * D].unsqueeze(1),
                                                          rden[p][:, j:j + 1], xb[p][:, j:j + 1, :], ALU.mult, ALU.add)
                last.then_inc(s["r"], 1)

            def norm1_a(b, p):
                dve.wait_ge(s["r"], made(b))
                statistics(k, dve, lambda j: k.spare[:, tile_of(b, j), :], stats1[p]).then_inc(s["stats1"], 1)

            def norm1_b(b, p):
                dve.wait_ge(s["stats1"], made(b))
                moments(k, dve, stats1[p], mv1[p]).then_inc(s["moments1"], 1)

            def norm1_x(b, p):
                dve.wait_ge(s["rstd1"], made(b))
                after(dve, s["x1T_p"], freed(b))
                after(dve, s["kept"], freed(b))
                for j in range(TPS):
                    last = normalise(nc, x1[p][:, j:j + 1, :], k.spare[:, tile_of(b, j), :], mv1[p], rstd1[p], j)
                last.then_inc(s["x1"], 1)

            def logits(b, p):
                dve.wait_ge(s["logits_p"], made(b))
                nc.vector.tensor_tensor(k.logits[:, bass.ds(b * TPS, TPS), :],
                                        x1_bank[:, SEQ:SEQ + TPS * E].rearrange("p (j e) -> p j e", j=TPS),
                                        k.row["b_router"][:, 0:TPS * E].rearrange("p (j e) -> p j e", j=TPS),
                                        ALU.add).then_inc(s["logits"], 1)

            pipeline(dve, [
                (1, norm_x), (4, mask), (6, norm1_x), (5, add), (0, norm_a), (3, features_of), (0, norm_b),
                (2, gate), (5, norm1_a), (2, values), (5, norm1_b), (4, denominators), (2, lows), (4, inverses),
                (6, logits)
            ])

        @block.tensor
        def _(pe):
            for name in "xnT_p qk_p gate_p v_p attn_p num_p proj_p x1T_p logits_p".split():
                credit(pe, s[name])
            pe.wait_ge(s_now, 16 * len(NOW))
            pe.wait_ge(s_set, 4)

            def norm_t(b, p):
                pe.wait_ge(s["xn"], made(b))
                pe.wait_ge(s["xnT"], made(b - 1))
                for j in range(TPS):
                    last = nc.tensor.transpose(t_bank[:, j * P:(j + 1) * P], xn[p][:, j, :], k.ident)
                last.then_inc(s["xnT_p"], 1)

            def project(b, p):
                pe.wait_ge(s["xnT"], made(b))
                pe.wait_ge(s["th"], made(b - 1))
                nc.tensor.matmul(gate_bank[:, 0:SEQ], k.w_qkvg[:, 3 * D:4 * D], xnT[p][:], start=True, stop=True
                                 ).then_inc(s["gate_p"], 1)
                pe.wait_ge(s["qk"], made(b - 1))
                nc.tensor.matmul(qk_bank[:, 0:SEQ], k.w_qkvg[:, 0:D], xnT[p][:], start=True, stop=True)
                nc.tensor.matmul(qk_bank[:, SEQ:2 * SEQ], k.w_qkvg[:, D:2 * D], xnT[p][:], start=True, stop=True
                                 ).then_inc(s["qk_p"], 1)
                pe.wait_ge(s["v"], made(b - 1))
                for j in range(TPS):
                    last = nc.tensor.matmul(v_bank[:, j * D:(j + 1) * D], xnT[p][:, j * P:(j + 1) * P],
                                            k.w_qkvg[:, 2 * D:3 * D], start=True, stop=True)
                last.then_inc(s["v_p"], 1)

            def attend(b, p):
                pe.wait_ge(s["features"], made(b))
                pe.wait_ge(s["attn"], made(b - 1))
                f = features[p]
                nc.tensor.matmul(attn_bank[:, 0:SEQ], f[:, SEQ:SEQ + P], f[:, 0:SEQ], start=True, stop=True)
                nc.tensor.matmul(attn_bank[:, SEQ:SEQ + P], f[:, SEQ + P:2 * SEQ], f[:, P:SEQ], start=True, stop=True
                                 ).then_inc(s["attn_p"], 1)

            def apply(b, p):
                pe.wait_ge(s["attn"], made(b))
                pe.wait_ge(s["v"], made(b))
                pe.wait_ge(s["rden0"], made(b - 1))
                nc.tensor.matmul(num_bank[:, 0:P], v[p][:, 0, :], attn[p][:, 0:P], start=True, stop=True)
                nc.tensor.matmul(num_bank[:, P:SEQ], v[p][:, 0, :], attn[p][:, P:SEQ], start=True, stop=False)
                nc.tensor.matmul(num_bank[:, P:SEQ], v[p][:, 1, :], attn[p][:, SEQ:SEQ + P], start=False, stop=True)
                nc.tensor.matmul(num_bank[:, SEQ:SEQ + 1], attn[p][:, 0:P], ones[:], start=True, stop=True)
                nc.tensor.matmul(num_bank[:, SEQ + 1:SEQ + 2], attn[p][:, P:SEQ], ones[:], start=True, stop=False)
                nc.tensor.matmul(num_bank[:, SEQ + 1:SEQ + 2], attn[p][:, SEQ:SEQ + P], ones[:], start=False, stop=True
                                 ).then_inc(s["num_p"], 1)

            def out(b, p):
                pe.wait_ge(s["numT"], made(b))
                pe.wait_ge(s["r"], made(b - 1))
                if isinstance(b, int) and b == 0:
                    pe.wait_ge(s_w, 16 * len(LATER))
                for j in range(TPS):
                    last = nc.tensor.matmul(proj_bank[:, j * D:(j + 1) * D], numT[p][:, j * P:(j + 1) * P], k.w_proj[:],
                                            start=True, stop=True)
                last.then_inc(s["proj_p"], 1)

            def turn(b, p):
                pe.wait_ge(s["x1"], made(b))
                pe.wait_ge(s["logits"], made(b - 1))
                for j in range(TPS):
                    last = nc.tensor.transpose(x1_bank[:, j * P:(j + 1) * P], x1[p][:, j, :], k.ident)
                last.then_inc(s["x1T_p"], 1)

            def logits(b, p):
                pe.wait_ge(s["x1T"], made(b))
                for j in range(TPS):
                    last = nc.tensor.matmul(x1_bank[:, SEQ + j * E:SEQ + (j + 1) * E], x1T[p][:, j * P:(j + 1) * P],
                                            k.w_router[:, 0, :], start=True, stop=True)
                last.then_inc(s["logits_p"], 1)

            pipeline(pe, [(5, out), (2, project), (1, norm_t), (4, apply), (6, turn), (3, attend), (6, logits)])


def router(k, c, layer):
    nc = k.nc
    full = [c.enter_context(nc.sbuf_tensor(f"rt{layer}_{i}", [P, TILES, E], F32)) for i in range(5)]
    few = [c.enter_context(nc.sbuf_tensor(f"rf{layer}_{i}", [P, TILES], F32)) for i in range(8)]
    shifted, probs, picked, rest, second = full
    top, total, best, next_best, place, w1, w2, scale = few
    s_step, s_shifted, s_exp, s_routed = (k.sem(f"rt_{name}{layer}") for name in "step shifted exp routed".split())
    rank = k.index_rank.rearrange("p (t e) -> p t e", t=TILES)

    def on_scalar(act):
        act.wait_ge(s_shifted, 1)
        nc.scalar.activation(probs[:], shifted[:], ACT.Exp).then_inc(s_exp, 1)

    def on_vector(dve):
        steps = [0]

        def step(instruction):
            instruction.then_inc(s_step, 1)
            steps[0] += 1
            return steps[0]

        def wait(value):
            dve.wait_ge(s_step, value)

        def largest(out, values):
            return step(nc.vector.tensor_reduce(out[:], values[:], AX, ALU.max))

        tops = largest(top, k.logits)
        wait(tops)
        nc.vector.tensor_tensor(shifted[:], k.logits[:], spread(top[:], E), ALU.subtract).then_inc(s_shifted, 1)
        dve.wait_ge(s_exp, 1)
        wait(step(nc.vector.tensor_reduce(total[:], probs[:], AX, ALU.add)))
        wait(step(nc.vector.reciprocal(total[:], total[:])))
        wait(step(nc.vector.tensor_tensor(probs[:], probs[:], spread(total[:], E), ALU.mult)))
        wait(largest(best, probs))
        wait(step(nc.vector.tensor_tensor(picked[:], probs[:], spread(best[:], E), ALU.is_equal)))
        wait(step(nc.vector.tensor_tensor(picked[:], picked[:], rank, ALU.mult)))
        wait(largest(place, picked))
        wait(step(nc.vector.tensor_tensor(picked[:], picked[:], spread(place[:], E), ALU.is_equal)))
        wait(step(nc.vector.scalar_tensor_tensor(rest[:], picked[:], -2.0, probs[:], ALU.mult, ALU.add)))
        wait(largest(next_best, rest))
        same = step(nc.vector.tensor_tensor(second[:], rest[:], spread(next_best[:], E), ALU.is_equal))
        both = step(nc.vector.tensor_tensor(scale[:], best[:], next_best[:], ALU.add))
        wait(same)
        ranked = step(nc.vector.tensor_tensor(second[:], second[:], rank, ALU.mult))
        wait(both)
        both = step(nc.vector.tensor_scalar(scale[:], scale[:], MOE_EPS if layer else TOPK_EPS, None, ALU.add))
        wait(ranked)
        ranked = largest(place, second)
        wait(both)
        scaled = step(nc.vector.reciprocal(scale[:], scale[:]))
        wait(ranked)
        chosen = step(nc.vector.tensor_tensor(second[:], second[:], spread(place[:], E), ALU.is_equal))
        wait(scaled)
        if layer == 0:
            step(nc.vector.tensor_tensor(w1[:], best[:], scale[:], ALU.mult))
            weights = step(nc.vector.tensor_tensor(w2[:], next_best[:], scale[:], ALU.mult))
        wait(chosen)
        chosen = step(nc.vector.tensor_tensor(picked[:], picked[:], second[:], ALU.add))
        if layer == 0:
            wait(weights)
            wait(step(nc.vector.tensor_tensor(w1[:], w1[:], w2[:], ALU.add)))
            clipped = step(nc.vector.tensor_scalar(w2[:], w1[:], TOPK_EPS, None, ALU.max))
            step(nc.vector.tensor_scalar(w1[:], w1[:], TOPK_EPS, 1.0, ALU.mult, ALU.add))
            wait(clipped)
            clipped = step(nc.vector.reciprocal(w2[:], w2[:]))
        wait(chosen)
        chosen = step(nc.vector.tensor_tensor(picked[:], picked[:], probs[:], ALU.mult))
        if layer == 0:
            wait(clipped)
            wait(step(nc.vector.tensor_tensor(w1[:], w1[:], w2[:], ALU.mult)))
            wait(step(nc.vector.tensor_tensor(scale[:], scale[:], w1[:], ALU.mult)))
        wait(chosen)
        out = k.cw_by_expert[:].rearrange("p e t -> p t e") if layer else k.cw[:]
        nc.vector.tensor_tensor(out, picked[:], spread(scale[:], E), ALU.mult).then_inc(s_routed, 1)

    return on_scalar, on_vector, s_routed


def layer0_experts(k):
    nc = k.nc
    with ExitStack() as c:
        sb = lambda name, shape: c.enter_context(nc.sbuf_tensor("e_" + name, shape, F32))
        pair = lambda name, shape: [sb(f"{name}{i}", shape) for i in range(2)]
        HALF = E // 2
        xc, xT = pair("xc", [P, TPS, D]), pair("xT", [P, SEQ])
        wy = pair("wy", [P, TPS, 2, HALF * D])
        quad, duo, one = pair("quad", [P, TPS, 4 * D]), pair("duo", [P, TPS, 2 * D]), pair("one", [P, TPS, D])
        r = pair("r", [P, TPS, D])
        stats, mv, rstd = pair("stats", [P, TPS, 6]), pair("mv", [P, TPS, 2]), pair("rstd", [P, TPS])
        t_bank, y_banks = k.psum[7], k.psum[0:4]
        names = "xc xT_p xT y_p wy_act wy_dve quad duo one r stats moments var rstd x2".split()
        s = {n: k.sem("e_" + n) for n in names}
        per = dict(y_p=TPS, wy_act=TPS, wy_dve=TPS)
        route_on_scalar, route_on_vector, s_routed = router(k, c, 0)
        block = c.enter_context(nc.Block(no_gpsimd_drain=True))

        @block.gpsimd
        def _(pool):
            for name in "xc duo one var rstd".split():
                credit(pool, s[name])

            def fetch(b, p):
                after(pool, s["xT_p"], freed(b))
                k.settle(pool)
                pool.tensor_copy(xc[p][:], k.x[:, bass.ds(b * TPS, TPS), :]).then_inc(s["xc"], 1)

            def add(b, p):
                pool.wait_ge(s["quad"], made(b))
                pool.tensor_tensor(duo[p][:], quad[p][:, :, 0:2 * D], quad[p][:, :, 2 * D:4 * D], ALU.add).then_inc(s["duo"], 1)
                pool.wait_ge(s["duo"], made(b))
                after(pool, s["r"], freed(b))
                pool.tensor_tensor(one[p][:], duo[p][:, :, 0:D], duo[p][:, :, D:2 * D], ALU.add).then_inc(s["one"], 1)

            def norm(b, p):
                pool.wait_ge(s["moments"], made(b))
                rstd_of(k, pool, b, rstd[p], mv[p], s["var"]).then_inc(s["rstd"], 1)

            pipeline(pool, [(5, norm), (0, fetch), (3, add)], head=1)

        @block.scalar
        def _(act):
            for name in ("xT", "wy_act"):
                credit(act, s[name], per.get(name, 1))
            route_on_scalar(act)

            def turned(b, p):
                act.wait_ge(s["xT_p"], made(b))
                after(act, s["y_p"], freed(b, TPS, TPS))
                nc.scalar.activation(xT[p][:], t_bank[:, 0:SEQ], ACT.Copy).then_inc(s["xT"], 1)

            def weigh(j):
                def stage(b, p):
                    if isinstance(b, int) and b == 0:
                        act.wait_ge(s_routed, 1)
                    after(act, s["quad"], freed(b))
                    act.wait_ge(s["y_p"], made(b, j + 1, TPS))
                    for e in range(HALF):
                        k.settle(act)
                        last = nc.scalar.activation(
                            wy[p][:, j, 0, e * D:(e + 1) * D].unsqueeze(1), y_banks[2 * j][:, e * D:(e + 1) * D].unsqueeze(1),
                            ACT.Copy, scale=k.cw[:, tile_of(b, j), e])
                    last.then_inc(s["wy_act"], 1)
                return stage

            pipeline(act, [(5, idle), (1, turned), (2, weigh(0)), (2, weigh(1))], head=1)

        @block.vector
        def _(dve):
            for name in "wy_dve quad r stats moments x2".split():
                credit(dve, s[name], per.get(name, 1))
            route_on_vector(dve)
            dve.wait_ge(s_routed, 1)

            def weigh(j):
                def stage(b, p):
                    after(dve, s["quad"], freed(b))
                    dve.wait_ge(s["y_p"], made(b, j + 1, TPS))
                    w = k.cw[:, tile_of(b, j), HALF:E].rearrange("p t e -> p (t e)")
                    nc.vector.tensor_tensor(wy[p][:, j, 1].rearrange("p (e d) -> p e d", d=D),
                                            y_banks[2 * j + 1][:].rearrange("p (e d) -> p e d", d=D), spread(w, D), ALU.mult
                                            ).then_inc(s["wy_dve"], 1)
                return stage

            def add(b, p):
                dve.wait_ge(s["wy_act"], made(b, TPS, TPS))
                dve.wait_ge(s["wy_dve"], made(b, TPS, TPS))
                after(dve, s["duo"], freed(b))
                nc.vector.tensor_tensor(quad[p][:], wy[p][:, :, 0], wy[p][:, :, 1], ALU.add).then_inc(s["quad"], 1)

            def residual(b, p):
                dve.wait_ge(s["one"], made(b))
                after(dve, s["x2"], freed(b))
                k.settle(dve)
                nc.vector.tensor_tensor(r[p][:], k.x[:, bass.ds(b * TPS, TPS), :], one[p][:], ALU.add).then_inc(s["r"], 1)

            def norm_a(b, p):
                dve.wait_ge(s["r"], made(b))
                statistics(k, dve, lambda j: r[p][:, j, :], stats[p]).then_inc(s["stats"], 1)

            def norm_b(b, p):
                dve.wait_ge(s["stats"], made(b))
                moments(k, dve, stats[p], mv[p]).then_inc(s["moments"], 1)

            def norm_x(b, p):
                dve.wait_ge(s["rstd"], made(b))
                for j in range(TPS):
                    last = normalise(nc, k.x[:, tile_of(b, j), :], r[p][:, j:j + 1, :], mv[p], rstd[p], j)
                last.then_inc(s["x2"], 1)

            pipeline(dve, [
                (3, add), (4, residual), (2, weigh(0)), (4, norm_a), (2, weigh(1)), (4, norm_b), (5, norm_x)
            ], head=1)

        @block.tensor
        def _(pe):
            for name in ("xT_p", "y_p"):
                credit(pe, s[name], per.get(name, 1))

            def turn(b, p):
                pe.wait_ge(s["xc"], made(b))
                pe.wait_ge(s["xT"], made(b - 1))
                for j in range(TPS):
                    last = nc.tensor.transpose(t_bank[:, j * P:(j + 1) * P], xc[p][:, j, :], k.ident)
                last.then_inc(s["xT_p"], 1)

            def experts(j):
                def stage(b, p):
                    pe.wait_ge(s["xT"], made(b))
                    pe.wait_ge(s["wy_act"], made(b - 1, j + 1, TPS))
                    pe.wait_ge(s["wy_dve"], made(b - 1, j + 1, TPS))
                    for h in range(2):
                        last = nc.tensor.matmul(y_banks[2 * j + h][:], xT[p][:, j * P:(j + 1) * P],
                                                k.w_exp0[:, h * 4 * D:(h + 1) * 4 * D], start=True, stop=True)
                    last.then_inc(s["y_p"], 1)
                return stage

            pipeline(pe, [(5, idle), (1, turn), (2, experts(0)), (2, experts(1))], head=1)


def statistics(k, dve, rows, st):
    k.settle(dve)
    for j in range(TPS):
        last = k.nc.vector.bn_stats(st[:, j, :], rows(j))
    return last


def moments(k, dve, st, m):
    k.settle(dve)
    for j in range(TPS):
        last = k.nc.vector.bn_aggr(m[:, j, :], st[:, j, :])
    return last


def rstd_of(k, pool, b, rs, m, s_var):
    k.settle(pool)
    pool.tensor_scalar(rs[:], m[:, :, 1], LN_EPS, None, ALU.add).then_inc(s_var, 1)
    pool.wait_ge(s_var, made(b))
    return pool.tensor_tensor(rs[:], rs[:], k.minus_half[:], ALU.pow)


def load_expert(k, sp, b, raw, s_raw):
    w13 = 2 * HID
    sp.dma_start(raw[:, 0:w13], k.dram["w13"][:, bass.ds(b * w13, w13)]).then_inc(s_raw, 16)
    for ch, (at, n) in enumerate(CHUNKS):
        sp.dma_start(raw[0:n, w13 + ch * D:w13 + (ch + 1) * D],
                     k.dram["w2"][at:at + n, bass.ds(b * D, D)]).then_inc(s_raw, 16)


def expert_parts(op):
    full = MOE_COLS - D
    op(slice(0, P), slice(0, full))
    return op(slice(0, CHUNKS[-1][1]), slice(full, MOE_COLS))


def normalise(nc, dst, src, m, rs, j):
    return nc.vector.tensor_scalar(dst, src, m[:, j, 0:1], rs[:, j:j + 1], ALU.subtract, ALU.mult)


def layer1_attention(k):
    nc = k.nc
    k.end_layer0()
    QUERY, KEY = 0, 1
    Q_NORM, K_NORM, USED = 3 * DH + 2, 3 * DH, 3 * DH + 4
    PART = 4
    PARTS = HEADS // PART
    D_BANKS = 3
    FILLS = 4
    with ExitStack() as c:
        sb = lambda name, shape, dt=F32: c.enter_context(nc.sbuf_tensor("s_" + name, shape, dt))
        pair = lambda name, shape, dt=F32: [sb(f"{name}{i}", shape, dt) for i in range(2)]
        stats, mv, rstd = pair("stats", [P, TPS, 6]), pair("mv", [P, TPS, 2]), pair("rstd", [P, TPS])
        xn, xnT = pair("xn", [P, TPS, D]), pair("xnT", [P, SEQ])
        qk = pair("qk", [P, TPS, 2, HEADS, DH])
        squares, norms = pair("squares", [P, TPS, 2, HEADS, DH]), pair("norms", [P, TPS, 2, HEADS])
        slots = pair("slots", [P, TPS, 2, HEADS, HW])
        slotsT = pair("slotsT", [P, 2 * GROUPS, TPS, P], F32R)
        values_all, gates = sb("values_all", [P, TILES, HEADS, DH]), k.spare
        values = pair("values", [P, TPS, HEADS, HW])
        w = pair("w", [P, HEADS, TPS * SEQ])
        avT = pair("avT", [P, GROUPS, SEQ])
        rden = pair("rden", [P, TPS, HEADS])
        o, xb, r = (pair(n, [P, TPS, D]) for n in ("o", "xb", "r"))
        oT = pair("oT", [P, SEQ])
        stats1, mv1, rstd1 = pair("stats1", [P, TPS, 6]), pair("mv1", [P, TPS, 2]), pair("rstd1", [P, TPS])
        x3, x3T = pair("x3", [P, TPS, D]), pair("x3T", [P, SEQ])
        eps = sb("eps", [P, 1])
        t_bank, p_bank, d_banks, avT_banks, out_bank = k.psum[0], k.psum[1], k.psum[2:5], k.psum[5:7], k.psum[7]
        av_banks = avT_banks[1], t_bank
        names = ("stats moments var rstd xn xnT_p xnT p_p qkvg high lows squares norms norms_high slots slots_p slotsT "
                 "d_p d dist logd w values avT_p avT av_p rden0 rden o0 o oT_p oT out_p xb0 xb r "
                 "stats1 moments1 var1 rstd1 x3 kept x3T_p x3T logits_p logits x_high x_low").split()
        s = {n: k.sem("h_" + n) for n in names}
        per = dict(p_p=TPS, qkvg=TPS, slots_p=FILLS, slotsT=FILLS, d_p=HEADS, d=HEADS, dist=PARTS, logd=PARTS,
                   w=PARTS, avT_p=2, avT=2)
        s_set, s_raw0, s_high0 = k.sem("h_set"), k.sem("h_raw0"), k.sem("h_high0")
        block = c.enter_context(nc.Block(no_gpsimd_drain=True))

        @block.gpsimd
        def _(pool):
            for name in "var rstd squares lows values xb0 xb o var1 rstd1 kept x_high x_low".split():
                credit(pool, s[name])
            pool.memset(eps[:], SHEP_EPS).then_inc(s_set, 1)

            def norm(b, p):
                pool.wait_ge(s["moments"], made(b))
                rstd_of(k, pool, b, rstd[p], mv[p], s["var"]).then_inc(s["rstd"], 1)

            def square(b, p):
                pool.wait_ge(s["qkvg"], made(b, TPS, TPS))
                after(pool, s["norms"], freed(b))
                pool.tensor_tensor(squares[p][:], qk[p][:], qk[p][:], ALU.mult).then_inc(s["squares"], 1)

            def lows(b, p):
                pool.wait_ge(s["high"], made(b))
                for q, at in ((QUERY, 2 * DH), (KEY, DH)):
                    last = pool.tensor_tensor(slots[p][:, :, q, :, at:at + DH], qk[p][:, :, q], slots[p][:, :, q, :, 0:DH],
                                              ALU.subtract)
                last.then_inc(s["lows"], 1)

            def place_values(b, p):
                if isinstance(b, int) and b < 2:
                    pool.memset(values[p][:, :, :, DH:], 1.0)
                after(pool, s["avT_p"], freed(b, 2, 2))
                k.settle(pool)
                pool.tensor_copy(values[p][:, :, :, 0:DH], values_all[:, bass.ds(b * TPS, TPS), :, :]).then_inc(s["values"], 1)

            def gate(b, p):
                pool.wait_ge(s["o0"], made(b))
                k.settle(pool)
                pool.tensor_tensor(o[p][:], o[p][:], gates[:, bass.ds(b * TPS, TPS), :], ALU.mult).then_inc(s["o"], 1)

            def residual(b, p):
                after(pool, s["r"], freed(b))
                k.settle(pool)
                for j in range(TPS):
                    last = pool.tensor_tensor(xb[p][:, j:j + 1, :], k.x[:, tile_of(b, j), :],
                                              k.row["b_out"].unsqueeze(1), ALU.add)
                last.then_inc(s["xb0"], 1)
                pool.wait_ge(s["xb0"], made(b))
                k.settle(pool)
                pool.tensor_tensor(xb[p][:], k.x[:, bass.ds(b * TPS, TPS), :], xb[p][:], ALU.add).then_inc(s["xb"], 1)

            def norm1(b, p):
                pool.wait_ge(s["moments1"], made(b))
                rstd_of(k, pool, b, rstd1[p], mv1[p], s["var1"]).then_inc(s["rstd1"], 1)

            def keep(b, p):
                pool.wait_ge(s["x3"], made(b))
                k.settle(pool)
                pool.tensor_copy(k.x[:, bass.ds(b * TPS, TPS), :], x3[p][:]).then_inc(s["kept"], 1)

            def split(b, p):
                pool.wait_ge(s["x3T"], made(b))
                k.settle(pool)
                cols = bass.ds(b * SEQ, SEQ)
                pool.tensor_copy(k.x_high[:, cols], x3T[p][:]).then_inc(s["x_high"], 1)
                pool.wait_ge(s["x_high"], made(b))
                k.settle(pool)
                pool.tensor_tensor(k.x_low[:, cols], x3T[p][:], k.x_high[:, cols].bitcast(F32), ALU.subtract
                                   ).then_inc(s["x_low"], 1)

            pipeline(pool, [
                (0, norm), (5, residual), (1, square), (3, place_values), (5, gate), (6, split), (1, lows),
                (5, norm1), (5, keep)
            ])
            pool.wait_ge(s["kept"], made(SEQS - 1))
            pool.wait_ge(s["x_low"], made(SEQS - 1))

        @block.scalar
        def _(act):
            for name in "dist logd w".split():
                credit(act, s[name], per.get(name, 1))
            act.wait_ge(s_set, 3)

            def weights(b, p):
                for n in range(PARTS):
                    part = w[p][:, n * PART:(n + 1) * PART, :]
                    act.wait_ge(s["d"], made(b, (n + 1) * PART, HEADS))
                    nc.scalar.activation(part, part, ACT.Sqrt).then_inc(s["dist"], 1)
                act.preload_act_table_set("natural_log_exp_and_others")
                for n in range(PARTS):
                    part = w[p][:, n * PART:(n + 1) * PART, :]
                    act.wait_ge(s["dist"], made(b, n + 1, PARTS))
                    nc.scalar.activation(part, part, ACT.Ln, bias=eps[:, 0:1]).then_inc(s["logd"], 1)
                for n in range(PARTS):
                    part = w[p][:, n * PART:(n + 1) * PART, :]
                    act.wait_ge(s["logd"], made(b, n + 1, PARTS))
                    nc.scalar.activation(part, part, ACT.Exp, scale=-2.0).then_inc(s["w"], 1)

            pipeline(act, [(3, weights), (6, idle)])
            act.wait_ge(s_raw0, 16 * (1 + len(CHUNKS)))
            expert_parts(lambda ps, cs: nc.scalar.activation(k.moe_high0[ps, cs], k.moe_raw0[ps, cs], ACT.Copy)
                         ).then_inc(s_high0, 1)
            act.wait_ge(s_high0, 1)

        @block.sync
        def _(sp):
            load_expert(k, sp, 0, k.moe_raw0, s_raw0)

        @block.vector
        def _(dve):
            for name in ("stats moments xn xnT qkvg high norms norms_high slots slotsT d avT rden0 rden o0 oT r stats1 "
                         "moments1 x3 x3T logits").split():
                credit(dve, s[name], per.get(name, 1))
            for t in slots:
                nc.vector.memset(t[:, :, :, :, 3 * DH:], -0.5).then_inc(s_set, 1)

            def norm_a(b, p):
                statistics(k, dve, lambda j: k.x[:, tile_of(b, j), :], stats[p]).then_inc(s["stats"], 1)

            def norm_b(b, p):
                dve.wait_ge(s["stats"], made(b))
                moments(k, dve, stats[p], mv[p]).then_inc(s["moments"], 1)

            def norm_x(b, p):
                dve.wait_ge(s["rstd"], made(b))
                after(dve, s["xnT_p"], freed(b))
                for j in range(TPS):
                    last = normalise(nc, xn[p][:, j:j + 1, :], k.x[:, tile_of(b, j), :], mv[p], rstd[p], j)
                last.then_inc(s["xn"], 1)

            def norm_t(b, p):
                dve.wait_ge(s["xnT_p"], made(b))
                after(dve, s["p_p"], freed(b, TPS, TPS))
                nc.vector.tensor_copy(xnT[p][:], t_bank[:, 0:SEQ]).then_inc(s["xnT"], 1)

            def build(j):
                def stage(b, p):
                    dve.wait_ge(s["p_p"], made(b, j + 1, TPS))
                    after(dve, s["lows"], freed(b))
                    after(dve, s["squares"], freed(b))
                    nc.vector.tensor_tensor(qk[p][:, j].rearrange("p q h w -> p (q h w)"), p_bank[:, 0:2 * D],
                                            k.row["b_in"][:, 0:2 * D], ALU.add)
                    nc.vector.tensor_tensor(values_all[:, tile_of(b, j), :, :].rearrange("p t h w -> p t (h w)"),
                                            p_bank[:, 2 * D:3 * D].unsqueeze(1),
                                            k.row["b_in"][:, 2 * D:3 * D].unsqueeze(1), ALU.add)
                    nc.vector.tensor_tensor(gates[:, tile_of(b, j), :], p_bank[:, 3 * D:4 * D].unsqueeze(1),
                                            k.row["b_in"][:, 3 * D:4 * D].unsqueeze(1), ALU.add).then_inc(s["qkvg"], 1)
                return stage

            def high(b, p):
                after(dve, s["slots_p"], freed(b, FILLS, FILLS))
                dve.wait_ge(s["qkvg"], made(b, TPS, TPS))
                nc.vector.tensor_copy(slots[p][:].rearrange("p j q h w -> p (j q h) w")[:, :, 0:DH].bitcast(F32R),
                                      qk[p][:].rearrange("p j q h w -> p (j q h) w"))
                for q, at in ((QUERY, DH), (KEY, 2 * DH)):
                    last = nc.vector.tensor_copy(slots[p][:, :, q, :, at:at + DH].bitcast(F32R), qk[p][:, :, q])
                last.then_inc(s["high"], 1)

            def norms_a(b, p):
                dve.wait_ge(s["squares"], made(b))
                nc.vector.tensor_reduce(norms[p][:].rearrange("p j q h -> p (j q h)"),
                                        squares[p][:].rearrange("p j q h w -> p (j q h) w"), AX, ALU.add).then_inc(s["norms"], 1)

            def norms_b(b, p):
                dve.wait_ge(s["norms"], made(b))
                for q, at in ((QUERY, Q_NORM), (KEY, K_NORM)):
                    last = nc.vector.tensor_copy(slots[p][:, :, q, :, at].bitcast(F32R), norms[p][:, :, q])
                last.then_inc(s["norms_high"], 1)

            def norms_c(b, p):
                dve.wait_ge(s["norms_high"], made(b))
                for q, at in ((QUERY, Q_NORM), (KEY, K_NORM)):
                    last = nc.vector.tensor_tensor(slots[p][:, :, q, :, at + 1], norms[p][:, :, q], slots[p][:, :, q, :, at],
                                                   ALU.subtract)
                last.then_inc(s["slots"], 1)

            def slots_t(f):
                def stage(b, p):
                    dve.wait_ge(s["slots_p"], made(b, f + 1, FILLS))
                    after(dve, s["d_p"], freed(b, HEADS, HEADS))
                    nc.vector.tensor_copy(slotsT[p][:, 2 * f:2 * f + 2].rearrange("p g j t -> p (g j t)"), t_bank[:]
                                          ).then_inc(s["slotsT"], 1)
                return stage

            def distances(h):
                def stage(b, p):
                    dve.wait_ge(s["d_p"], made(b, h + 1, HEADS))
                    nc.vector.tensor_scalar(w[p][:, h, :], d_banks[h % D_BANKS][:], -2.0, 0.0, ALU.mult, ALU.max
                                            ).then_inc(s["d"], 1)
                return stage

            def applied(half):
                def stage(b, p):
                    dve.wait_ge(s["avT_p"], made(b, half + 1, 2))
                    after(dve, s["av_p"], freed(b))
                    nc.vector.tensor_copy(avT[p][:, 2 * half:2 * half + 2].rearrange("p g t -> p (g t)"),
                                          avT_banks[half][:]).then_inc(s["avT"], 1)
                return stage

            av = [bank[:].rearrange("p (h w) -> p h w", w=HW) for bank in av_banks]

            def divide_a(b, p):
                dve.wait_ge(s["av_p"], made(b))
                for t in range(TPS):
                    last = nc.vector.tensor_scalar(rden[p][:, t], av[t][:, :, DH], SHEP_EPS, None, ALU.add)
                last.then_inc(s["rden0"], 1)

            def divide_b(b, p):
                dve.wait_ge(s["rden0"], made(b))
                nc.vector.reciprocal(rden[p][:], rden[p][:]).then_inc(s["rden"], 1)

            def divide_c(b, p):
                dve.wait_ge(s["rden"], made(b))
                after(dve, s["oT_p"], freed(b))
                for t in range(TPS):
                    last = nc.vector.tensor_tensor(o[p][:, t].rearrange("p (h w) -> p h w", w=DH), av[t][:, :, 0:DH],
                                                   spread(rden[p][:, t], DH), ALU.mult)
                last.then_inc(s["o0"], 1)

            def out_t(b, p):
                dve.wait_ge(s["oT_p"], made(b))
                after(dve, s["out_p"], freed(b))
                nc.vector.tensor_copy(oT[p][:], out_bank[:, 0:SEQ]).then_inc(s["oT"], 1)

            def add(b, p):
                dve.wait_ge(s["out_p"], made(b))
                dve.wait_ge(s["xb"], made(b))
                nc.vector.tensor_tensor(r[p][:], out_bank[:, SEQ:2 * SEQ].rearrange("p (j d) -> p j d", j=TPS), xb[p][:],
                                        ALU.add).then_inc(s["r"], 1)

            def norm1_a(b, p):
                dve.wait_ge(s["r"], made(b))
                statistics(k, dve, lambda j: r[p][:, j, :], stats1[p]).then_inc(s["stats1"], 1)

            def norm1_b(b, p):
                dve.wait_ge(s["stats1"], made(b))
                moments(k, dve, stats1[p], mv1[p]).then_inc(s["moments1"], 1)

            def norm1_x(b, p):
                dve.wait_ge(s["rstd1"], made(b))
                after(dve, s["x3T_p"], freed(b))
                after(dve, s["kept"], freed(b))
                for j in range(TPS):
                    last = normalise(nc, x3[p][:, j:j + 1, :], r[p][:, j:j + 1, :], mv1[p], rstd1[p], j)
                last.then_inc(s["x3"], 1)

            def norm1_t(b, p):
                dve.wait_ge(s["x3T_p"], made(b))
                after(dve, s["logits_p"], freed(b))
                after(dve, s["x_low"], freed(b))
                nc.vector.tensor_copy(x3T[p][:], out_bank[:, 0:SEQ]).then_inc(s["x3T"], 1)

            def logits(b, p):
                dve.wait_ge(s["logits_p"], made(b))
                nc.vector.tensor_copy(k.logits[:, bass.ds(b * TPS, TPS), :],
                                      out_bank[:, SEQ:SEQ + TPS * E].rearrange("p (j e) -> p j e", j=TPS)
                                      ).then_inc(s["logits"], 1)

            pipeline(dve, among_heads(lambda h: (2, distances(h)), {
                0: [(5, applied(1)), (6, norm1_t), (1, build(0)), (5, divide_a)], 1: [(0, norm_a)],
                2: [(5, divide_b)], 3: [(0, norm_b)],
                4: [(1, build(1)), (0, norm_x), (6, logits), (5, divide_c)],
                6: [(1, high), (1, norms_a), (4, applied(0))], 9: [(5, out_t), (1, norms_b)],
                10: [(1, norms_c), (0, norm_t), (1, slots_t(0))], 12: [(1, slots_t(1))],
                13: [(5, add), (1, slots_t(2))], 14: [(5, norm1_a), (5, norm1_b)],
                15: [(1, slots_t(3)), (5, norm1_x)]
            }))

        @block.tensor
        def _(pe):
            for name in "xnT_p p_p slots_p d_p avT_p av_p oT_p out_p x3T_p logits_p".split():
                credit(pe, s[name], per.get(name, 1))
            pe.wait_ge(s_set, 3)

            def norm_t(b, p):
                pe.wait_ge(s["xn"], made(b))
                pe.wait_ge(s["xnT"], made(b - 1))
                if not isinstance(b, int) or b >= 5:
                    pe.wait_ge(s["o0"], made(b - 5))
                after(pe, s["slotsT"], made(b - 1, 0, FILLS))
                for j in range(TPS):
                    last = nc.tensor.transpose(t_bank[:, j * P:(j + 1) * P], xn[p][:, j, :], k.ident)
                last.then_inc(s["xnT_p"], 1)

            def project(j):
                def stage(b, p):
                    pe.wait_ge(s["xnT"], made(b))
                    after(pe, s["qkvg"], made(b, j, TPS))
                    nc.tensor.matmul(p_bank[:], xnT[p][:, j * P:(j + 1) * P], k.w_in[:], start=True, stop=True
                                     ).then_inc(s["p_p"], 1)
                return stage

            def slots_t(f):
                def stage(b, p):
                    pe.wait_ge(s["slots"], made(b))
                    pe.wait_ge(s["lows"], made(b))
                    after(pe, s["slotsT"], made(b, f, FILLS))
                    pe.wait_ge(s["xnT"], made(b + 1) if not isinstance(b, int) or b + 1 < SEQS else made(b))
                    for g in range(2):
                        q, first = divmod((2 * f + g) * HG, HEADS)
                        for j in range(TPS):
                            last = nc.tensor.transpose(
                                t_bank[:, (g * TPS + j) * P:(g * TPS + j + 1) * P],
                                slots[p][:, j, q, first:first + HG, :].rearrange("p h w -> p (h w)"), k.ident)
                    last.then_inc(s["slots_p"], 1)
                return stage

            def distances(h):
                def stage(b, p):
                    if h == 0:
                        pe.wait_ge(s["slotsT"], made(b, FILLS, FILLS))
                    g, at = h // HG, h % HG * HW
                    before = [i for i in range(h - HEADS, h) if i % HEADS % D_BANKS == h % D_BANKS][-1]
                    after(pe, s["d"], made(b, before + 1, HEADS))
                    for kt in range(TPS):
                        last = nc.tensor.matmul(d_banks[h % D_BANKS][:, kt * SEQ:(kt + 1) * SEQ],
                                                slotsT[p][at:at + USED, GROUPS + g, kt, :],
                                                slotsT[p][at:at + USED, g, :, :].rearrange("p j t -> p (j t)"),
                                                start=True, stop=True)
                    last.then_inc(s["d_p"], 1)
                return stage

            def apply(h):
                half, g, at = h // (HEADS // 2), h // HG, h % HG * HW

                def stage(b, p):
                    if h % PART == 0:
                        pe.wait_ge(s["w"], made(b, h // PART + 1, PARTS))
                    if h == 0:
                        pe.wait_ge(s["values"], made(b))
                    if h % (HEADS // 2) == 0:
                        after(pe, s["avT"], made(b - 1, half + 1, 2))
                    if h == HEADS // 2:
                        pe.wait_ge(s["o0"], made(b - 1))
                    for kt in range(TPS):
                        last = nc.tensor.matmul(avT_banks[half][at:at + HW, g % 2 * SEQ:(g % 2 + 1) * SEQ],
                                                values[p][:, kt, h, :], w[p][:, h, kt * SEQ:(kt + 1) * SEQ],
                                                start=(kt == 0), stop=(kt == TPS - 1), tile_position=(0, at))
                    if h % (HEADS // 2) == HEADS // 2 - 1:
                        last.then_inc(s["avT_p"], 1)
                return stage

            def av_t(b, p):
                pe.wait_ge(s["avT"], made(b, 2, 2))
                behind = b + 3 if not isinstance(b, int) else min(b + 3, SEQS - 1)
                pe.wait_ge(s["slotsT"], made(behind, FILLS, FILLS))
                for t in range(TPS):
                    for g in range(GROUPS):
                        last = nc.tensor.transpose(av_banks[t][:, g * P:(g + 1) * P], avT[p][:, g, t * P:(t + 1) * P], k.ident)
                last.then_inc(s["av_p"], 1)

            def out_t(b, p):
                pe.wait_ge(s["o"], made(b))
                pe.wait_ge(s["logits"], made(b - 1))
                for j in range(TPS):
                    last = nc.tensor.transpose(out_bank[:, j * P:(j + 1) * P], o[p][:, j, :], k.ident)
                last.then_inc(s["oT_p"], 1)

            def out(b, p):
                pe.wait_ge(s["oT"], made(b))
                for j in range(TPS):
                    last = nc.tensor.matmul(out_bank[:, SEQ + j * D:SEQ + (j + 1) * D], oT[p][:, j * P:(j + 1) * P],
                                            k.w_out[:], start=True, stop=True)
                last.then_inc(s["out_p"], 1)

            def norm1_t(b, p):
                pe.wait_ge(s["x3"], made(b))
                for j in range(TPS):
                    last = nc.tensor.transpose(out_bank[:, j * P:(j + 1) * P], x3[p][:, j, :], k.ident)
                last.then_inc(s["x3T_p"], 1)

            def logits(b, p):
                pe.wait_ge(s["x3T"], made(b))
                pe.wait_ge(s["r"], made(b))
                for j in range(TPS):
                    at = SEQ + j * E
                    last = nc.tensor.matmul(out_bank[:, at:at + E], x3T[p][:, j * P:(j + 1) * P], k.w_router[:, 1, :],
                                            start=True, stop=True)
                last.then_inc(s["logits_p"], 1)

            pipeline(pe, among_heads(lambda h: [(4, apply(h)), (2, distances(h))], {
                0: [(1, project(0)), (6, norm1_t), (5, av_t)], 3: [(6, logits)], 4: [(1, project(1))],
                8: [(5, out_t)], 11: [(0, norm_t), (5, out), (1, slots_t(0))], 12: [(1, slots_t(1))],
                15: [(1, slots_t(2)), (1, slots_t(3))]
            }))


def layer1_moe(k):
    nc = k.nc
    BLOCK = 512
    BLOCKS, NCH = TOKENS // BLOCK, len(CHUNKS)
    UNITS = BLOCKS * NCH
    W13 = 2 * HID
    RING = 3
    CAST, LOW, DOWN = 1, 1, 2
    CUT = NCH
    TURN, ADD, MOMENTS, NORM = 0, 1, 2, 3

    def complete(q):
        return (q * SEQ // BLOCK + 2) * NCH + 1 + q % TPS

    with ExitStack() as c:
        sb = lambda name, shape, dt=F32: c.enter_context(nc.sbuf_tensor("m_" + name, shape, dt))
        pair = lambda name, shape, dt=F32: [sb(f"{name}{i}", shape, dt) for i in range(2)]
        ring = lambda name, shape, dt=F32: [sb(f"{name}{i}", shape, dt) for i in range(RING)]
        raw, high = [k.moe_raw0, sb("raw1", [P, MOE_COLS])], [k.moe_high0, sb("high1", [P, MOE_COLS], F32R)]
        low = pair("low", [P, MOE_COLS], F32R)
        share = pair("share", [P, TOKENS])
        silu, h = ring("silu", [P, BLOCK]), ring("h", [P, BLOCK])
        h_high, h_low = ring("h_high", [P, BLOCK], F32R), ring("h_low", [P, BLOCK], F32R)
        wy = pair("wy", [P, BLOCK])
        yT = k.yT
        cwT = sb("cwT", [P, P])
        shares = nc.dram_tensor("shares", [E, TILES, P], F32).ap()
        gate_banks, up_banks, y_banks = k.psum[0:2], k.psum[2:4], k.psum[4:6]
        names = "raw0 raw1 share0 share1 high low gate_p up_p silu h h_high h_low h_read wy yT".split()
        s = {n: k.sem("m_" + n) for n in names}
        per = {n: UNITS for n in "gate_p up_p silu h h_high h_low h_read".split()} | dict(wy=BLOCKS, yT=BLOCKS)
        s_cwT_p, s_cwT, s_shares = k.sem("m_cwT_p"), k.sem("m_cwT"), k.sem("m_shares")
        r, out = pair("r", [P, TPS, D]), pair("out", [P, TPS, D])
        stats, mv, rstd = pair("stats", [P, TPS, 6]), pair("mv", [P, TPS, 2]), pair("rstd", [P, TPS])
        out_dram, out_banks = k.out.rearrange("b (j p) d -> p (b j) d", p=P), k.psum[6:8]
        f = {n: k.sem("f_" + n) for n in "y_p r stats moments var rstd out".split()}
        f_stored = [k.sem(f"f_stored{p}") for p in range(2)]
        route_on_scalar, route_on_vector, s_routed = router(k, c, 1)
        block = c.enter_context(nc.Block(no_gpsimd_drain=True))

        def products(work, finish=()):
            most = max(lag for lag, _ in work)

            def stage(b, p, units):
                for u in units:
                    for lag, step in work:
                        if u >= lag:
                            step(b, p, u - lag)
                        elif not isinstance(b, int) or b > 0:
                            step(b - 1, 1 - p, UNITS + u - lag)
                    if isinstance(b, int) and b == E - 1:
                        finishing(u)

            def finishing(u):
                for lag, step in finish:
                    for q in range(SEQS):
                        if complete(q) + lag == u:
                            step(q, q % 2)

            def rest():
                for u in range(complete(SEQS - 1) + NORM + 1 - UNITS):
                    for lag, step in work:
                        if u < lag:
                            step(E - 1, (E - 1) % 2, UNITS + u - lag)
                    finishing(UNITS + u)
            return (lambda b, p: stage(b, p, range(CUT))), (lambda b, p: stage(b, p, range(CUT, UNITS))), rest

        @block.sync
        def _(sp):
            for name in "raw0 raw1 share0 share1".split():
                sp.sem_inc(s[name], 1 + 16 * (1 + NCH) if name == "raw0" else 1)

            def fetch(b, p):
                if isinstance(b, int) and b == 0:
                    return
                after(sp, s["low"], freed(b))
                load_expert(k, sp, b, raw[p], s[f"raw{p}"])

            def fetch_share(b, p):
                if isinstance(b, int) and b == 0:
                    sp.wait_ge(s_cwT, 1)
                    sp.dma_start(shares.rearrange("e t p -> (e t) p"), cwT[:]).then_inc(s_shares, 16)
                    sp.wait_ge(s_shares, 16)
                after(sp, s["wy"], freed(b, BLOCKS, BLOCKS))
                row = shares[bass.ds(b, 1)].rearrange("e t p -> e (t p)")
                sp.dma_start(share[p][:], row.to_broadcast([P, TOKENS])).then_inc(s[f"share{p}"], 16)

            pipeline(sp, [(0, fetch), (1, fetch_share), (2, idle)], E, 2)
            for q in range(SEQS):
                sp.wait_ge(f["out"], made(q))
                sp.dma_start(out_dram[:, q * TPS:(q + 1) * TPS, :], out[q % 2][:]).then_inc(f_stored[q % 2], 16)
            for p in range(2):
                sp.wait_ge(f_stored[p], 16 * SEQS // 2)

        @block.gpsimd
        def _(pool):
            for name in ("low", "yT"):
                credit(pool, s[name], per.get(name, 1))
            for name in ("var", "rstd"):
                credit(pool, f[name])

            def split(b, p):
                pool.wait_ge(s["high"], made(b))
                after(pool, s["h_read"], freed(b, UNITS, UNITS))
                expert_parts(lambda ps, cs: pool.tensor_tensor(
                    low[p][ps, cs], raw[p][ps, cs], high[p][ps, cs].bitcast(F32), ALU.subtract)).then_inc(s["low"], 1)

            def add(b, blocks):
                for t in blocks:
                    pool.wait_ge(s["wy"], made(b, t + 1, BLOCKS))
                    after(pool, s["yT"], made(b - 1, t + 1, BLOCKS))
                    cols = slice(t * BLOCK, (t + 1) * BLOCK)
                    pool.tensor_tensor(yT[:, cols], yT[:, cols], wy[t % 2][:], ALU.add).then_inc(s["yT"], 1)

            def norm(q, p):
                pool.wait_ge(f["moments"], made(q))
                rstd_of(k, pool, q, rstd[p], mv[p], f["var"]).then_inc(f["rstd"], 1)

            def add_rest(b, p):
                if not isinstance(b, int) or b < E - 1:
                    return add(b, range(1, BLOCKS))
                for t in range(1, BLOCKS + 1):
                    add(b, range(t, min(t + 1, BLOCKS)))
                    for q in range((t - 1) * BLOCK // SEQ, t * BLOCK // SEQ):
                        norm(q, q % 2)

            pipeline(pool, [(2, lambda b, p: add(b, range(1))), (1, split), (2, add_rest)], E, 2)
            pool.wait_ge(f["rstd"], made(SEQS - 1))

        @block.scalar
        def _(act):
            for name in ("high", "silu", "h_high"):
                credit(act, s[name], per.get(name, 1))
            route_on_scalar(act)

            def split(b, p):
                if isinstance(b, int) and b == 0:
                    return act.sem_inc(s["high"], 1)
                act.wait_ge(s[f"raw{p}"], landed(b, p, 1 + NCH))
                after(act, s["h_read"], freed(b, UNITS, UNITS))
                expert_parts(lambda ps, cs: nc.scalar.activation(high[p][ps, cs], raw[p][ps, cs], ACT.Copy)
                             ).then_inc(s["high"], 1)

            def gate(b, p, u):
                n = CHUNKS[u % NCH][1]
                act.wait_ge(s["gate_p"], made(b, u + 1, UNITS))
                after(act, s["h"], made(b, u + 1 - RING, UNITS))
                nc.scalar.activation(silu[u % RING][0:n, :], gate_banks[u % 2][0:n, :], ACT.Silu).then_inc(s["silu"], 1)

            def cast(b, p, u):
                n = CHUNKS[u % NCH][1]
                act.wait_ge(s["h"], made(b, u + 1, UNITS))
                after(act, s["h_read"], made(b, u + 1 - RING, UNITS))
                nc.scalar.activation(h_high[u % RING][0:n, :], h[u % RING][0:n, :], ACT.Copy).then_inc(s["h_high"], 1)

            begin, go_on, rest = products([(0, gate), (CAST, cast)])
            pipeline(act, [(2, begin), (1, split), (2, go_on)], E, 2)
            rest()

        @block.vector
        def _(dve):
            for name in ("h", "h_low", "wy"):
                credit(dve, s[name], per.get(name, 1))
            for name in ("r", "stats", "moments", "out"):
                credit(dve, f[name])
            route_on_vector(dve)

            def multiply(b, p, u):
                n = CHUNKS[u % NCH][1]
                if isinstance(b, int) and b == 0 and u == 1:
                    dve.wait_ge(s_cwT_p, 1)
                    nc.vector.tensor_copy(cwT[:], k.psum[6][:, 0:P]).then_inc(s_cwT, 1)
                dve.wait_ge(s["silu"], made(b, u + 1, UNITS))
                dve.wait_ge(s["up_p"], made(b, u + 1, UNITS))
                after(dve, s["h_high"], made(b, u + 1 - RING, UNITS))
                nc.vector.tensor_tensor(h[u % RING][0:n, :], up_banks[u % 2][0:n, :], silu[u % RING][0:n, :], ALU.mult
                                        ).then_inc(s["h"], 1)

            def split(b, p, u):
                n = CHUNKS[u % NCH][1]
                dve.wait_ge(s["h_high"], made(b, u + 1, UNITS))
                after(dve, s["h_read"], made(b, u + 1 - RING, UNITS))
                nc.vector.tensor_tensor(h_low[u % RING][0:n, :], h[u % RING][0:n, :], h_high[u % RING][0:n, :].bitcast(F32),
                                        ALU.subtract).then_inc(s["h_low"], 1)

            def weigh(b, p, u):
                if u % NCH < NCH - 1:
                    return
                t = u // NCH
                dve.wait_ge(s["h_read"], made(b, u + 1, UNITS))
                dve.wait_ge(s[f"share{p}"], landed(b, p))
                after(dve, s["yT"], made(b, t - 1, BLOCKS))
                nc.vector.tensor_tensor(wy[t % 2][:], y_banks[t % 2][:], share[p][:, t * BLOCK:(t + 1) * BLOCK], ALU.mult
                                        ).then_inc(s["wy"], 1)

            def sum_up(q, p):
                dve.wait_ge(f["y_p"], made(q))
                after(dve, f["out"], freed(q))
                nc.vector.tensor_tensor(r[p][:], out_banks[p][:, 0:SEQ].rearrange("p (j d) -> p j d", j=TPS),
                                        k.x[:, q * TPS:(q + 1) * TPS, :], ALU.add).then_inc(f["r"], 1)
                dve.wait_ge(f["r"], made(q))
                statistics(k, dve, lambda j: r[p][:, j, :], stats[p]).then_inc(f["stats"], 1)

            def moments_of(q, p):
                dve.wait_ge(f["stats"], made(q))
                moments(k, dve, stats[p], mv[p]).then_inc(f["moments"], 1)

            def norm(q, p):
                dve.wait_ge(f["rstd"], made(q))
                if q >= 2:
                    dve.wait_ge(f_stored[p], 16 * (q // 2))
                for j in range(TPS):
                    last = normalise(nc, out[p][:, j:j + 1, :], r[p][:, j:j + 1, :], mv[p], rstd[p], j)
                last.then_inc(f["out"], 1)

            begin, go_on, rest = products([(0, multiply), (LOW, split), (DOWN + 1, weigh)],
                                          [(ADD, sum_up), (MOMENTS, moments_of), (NORM, norm)])
            pipeline(dve, [(2, begin), (2, go_on)], E, 2)
            rest()

        @block.tensor
        def _(pe):
            for name in ("gate_p", "up_p", "h_read"):
                credit(pe, s[name], per.get(name, 1))
            credit(pe, f["y_p"])

            def product(out, at, n, cols, rows, parts, start, stop):
                for i, (w, x) in enumerate(parts):
                    last = nc.tensor.matmul(out, w[0:rows, at:at + n], x[0:rows, cols], start=start and i == 0,
                                            stop=stop and i == len(parts) - 1)
                return last

            def up(b, p, u):
                ch, t = u % NCH, u // NCH
                at, n = CHUNKS[ch]
                cols = slice(t * BLOCK, (t + 1) * BLOCK)
                parts = [(high[p], k.x_high), (high[p], k.x_low), (low[p], k.x_high)]
                if isinstance(b, int) and b == 0 and u == 1:
                    pe.wait_ge(s_routed, 1)
                    nc.tensor.transpose(k.psum[6][:, 0:P], k.cw_by_expert[:].rearrange("p e t -> p (e t)"), k.ident
                                        ).then_inc(s_cwT_p, 1)
                pe.wait_ge(s["low"], made(b))
                after(pe, s["silu"], made(b, u - 1, UNITS))
                product(gate_banks[u % 2][0:n, :], at, n, cols, P, parts, True, True).then_inc(s["gate_p"], 1)
                after(pe, s["h"], made(b, u - 1, UNITS))
                product(up_banks[u % 2][0:n, :], HID + at, n, cols, P, parts, True, True).then_inc(s["up_p"], 1)

            def down(b, p, u):
                ch, t = u % NCH, u // NCH
                n = CHUNKS[ch][1]
                pe.wait_ge(s["h_low"], made(b, u + 1, UNITS))
                if ch == 0:
                    after(pe, s["wy"], made(b, t - 1, BLOCKS))
                parts = [(high[p], h_high[u % RING]), (high[p], h_low[u % RING]), (low[p], h_high[u % RING])]
                last = product(y_banks[t % 2][:], W13 + ch * D, D, slice(0, BLOCK), n, parts, ch == 0, ch == NCH - 1)
                last.then_inc(s["h_read"], 1)

            def turn(q, p):
                pe.wait_ge(s["yT"], made(E - 1, q * SEQ // BLOCK + 1, BLOCKS))
                after(pe, f["r"], freed(q))
                for j in range(TPS):
                    at = (q * TPS + j) * P
                    last = nc.tensor.transpose(out_banks[p][:, j * P:(j + 1) * P], yT[:, at:at + P], k.ident)
                last.then_inc(f["y_p"], 1)

            begin, go_on, rest = products([(0, up), (DOWN, down)], [(TURN, turn)])
            pipeline(pe, [(2, begin), (2, go_on)], E, 2)
            rest()


def build(nc, dram, out):
    with ExitStack() as ctx:
        k = Kernel(nc, ctx, dram, out)
        layer0_attention(k)
        layer0_experts(k)
        layer1_attention(k)
        layer1_moe(k)




def layouts(i):
    import numpy as np

    f = lambda n: np.asarray(i[n])
    b_qkv = f("L0_attn_b_qkv").reshape(3, D)
    cols = np.stack([b_qkv[0], b_qkv[1], f("L0_attn_b_gate"), f("L0_attn_ln_g"), f("L0_attn_ln_b")] + [np.zeros(D, np.float32)] * 3, 1)
    order = np.arange(4 * D).reshape(HEADS, 4, DH).transpose(1, 0, 2).reshape(-1)
    rows = [np.concatenate([b_qkv[2]] * TPS), f("L0_attn_b_proj"), np.concatenate([f("L0_ffn_router_b")] * TILES),
            f("L1_attn_b_in")[order], f("L1_attn_b_out")]
    t = np.arange(P)
    causal = (t[:, None] <= t[None, :]).astype(np.float32)
    rank = np.broadcast_to(np.tile(np.arange(E, 0, -1, dtype=np.float32), TILES), (P, TILES * E))
    return {
        "x": f("L0_attn_x"),
        "consts": np.concatenate([np.eye(P, dtype=np.float32), causal, np.ones((P, P), np.float32), causal, rank], 1),
        "cols": cols,
        "rows": np.broadcast_to(np.concatenate(rows), (P, sum(n for _, n in ROWS))),
        "w_qkvg": np.concatenate([f("L0_attn_w_qkv"), f("L0_attn_w_gate")], 1),
        "w_proj": f("L0_attn_w_proj"),
        "w_router": np.stack([f("L0_ffn_router_w").T, f("L1_ffn_Wg").T], 1),
        "w_exp0": f("L0_ffn_expert_weights").transpose(1, 0, 2).reshape(D, E * D),
        "w_in": f("L1_attn_W_in").T[:, order],
        "w_out": f("L1_attn_W_out").T,
        "w13": np.concatenate([f("L1_ffn_W1"), f("L1_ffn_W3")], 1).transpose(2, 0, 1).reshape(D, E * 2 * HID),
        "w2": f("L1_ffn_W2").transpose(2, 0, 1).reshape(HID, E * D),
    }


def kernel(**inputs):
    import numpy as np
    import concourse.bacc as bacc
    from concourse.bass_utils import run_bass_kernel_spmd

    arrays = {name: np.ascontiguousarray(a) for name, a in layouts(inputs).items()}
    nc = bacc.Bacc("TRN2", target_bir_lowering=False, num_devices=1)
    dram = {name: nc.dram_tensor(name, a.shape, F32, kind="ExternalInput").ap() for name, a in arrays.items()}
    out = nc.dram_tensor("out", (SEQS, SEQ, D), F32, kind="ExternalOutput").ap()
    build(nc, dram, out)
    r = run_bass_kernel_spmd(nc, [arrays], core_ids=[0])
    return r.results[0]["out"]
```
